# Optimizing a Trainium2 kernel written in Bass

```python
import numpy as np
import jax
import jax.numpy as jnp

def _softmax(x, axis=-1):
    return jax.nn.softmax(x, axis=axis)

def _gelu(x):
    return jax.nn.gelu(x, approximate=True)

def _silu(x):
    return jax.nn.silu(x)

def _sigmoid(x):
    return jax.nn.sigmoid(x)

def _layernorm(x, axis=-1, eps=1e-05):
    m = jnp.mean(x, axis=axis, keepdims=True)
    v = jnp.var(x, axis=axis, keepdims=True)
    return (x - m) / jnp.sqrt(v + eps)

def _scatter_add(tgt, idx, src, axis=0):
    return tgt.at[idx].add(src)

def _segment_sum(src, seg, n):
    return jax.ops.segment_sum(src, seg, n)
kernel_name = 'mk_adaln_d2_jaxref_r8_8b3d2b'

def setup_inputs(seed: int=0):
    np.random.seed(seed)
    _w = jnp.asarray

    def _L0_attn_setup():
        import jax, jax.numpy as jnp
        import numpy as np
        EPS = 1e-08

        def rmsnorm(x, w):
            norm = jax.lax.rsqrt(jnp.mean(x * x, axis=-1, keepdims=True) + EPS)
            return x * norm * w
        key = jax.random.key(seed)
        ks = jax.random.split(key, 10)
        B, L, D, S = (8, 512, 128, 32)
        sD = 1.0 / np.sqrt(D)
        sS = 1.0 / np.sqrt(S)
        return {'x': jax.random.normal(ks[0], (B, L, D), jnp.float32), 'w_norm': jnp.ones((D,), jnp.float32), 'W_in': jax.random.normal(ks[1], (D, 3 * S), jnp.float32) * sD, 'b_in': jnp.zeros((3 * S,), jnp.float32), 'W_x': jax.random.normal(ks[2], (S, S), jnp.float32) * sS, 'b_x': jnp.zeros((S,), jnp.float32), 'W_dt': jax.random.normal(ks[3], (S, S), jnp.float32) * sS, 'b_dt': jnp.zeros((S,), jnp.float32), 'W_out': jax.random.normal(ks[4], (S, D), jnp.float32) * sS, 'b_out': jnp.zeros((D,), jnp.float32)}
    _L0_attn_in = _L0_attn_setup()

    def _L0_ffn_setup():
        import jax, jax.numpy as jnp
        import numpy as np
        DIM = 128

        def _reference_tuple_inner(x, W_r, W_k, W_v, mu_r, mu_k):
            B, T, C = x.shape
            x_prev = jnp.concatenate([jnp.zeros((B, 1, C), x.dtype), x[:, :-1, :]], axis=1)
            xr = mu_r * x + (1.0 - mu_r) * x_prev
            xk = mu_k * x + (1.0 - mu_k) * x_prev
            r = jax.nn.sigmoid(jnp.einsum('btc,dc->btd', xr, W_r))
            k = jnp.einsum('btc,dc->btd', xk, W_k)
            k_act = jnp.square(jax.nn.relu(k))
            out = r * jnp.einsum('btc,dc->btd', k_act, W_v)
            new_state = x[:, -1, :]
            return (out, new_state)
        key = jax.random.key(seed)
        ks = jax.random.split(key, 6)
        B, T, C = (8, 256, DIM)
        x = jax.random.normal(ks[0], (B, T, C), dtype=jnp.float32)
        s = 1.0 / np.sqrt(C)
        W_r = jax.random.uniform(ks[1], (C, C), jnp.float32, -s, s)
        W_k = jax.random.uniform(ks[2], (C, C), jnp.float32, -s, s)
        W_v = jax.random.uniform(ks[3], (C, C), jnp.float32, -s, s)
        mu_r = jax.random.uniform(ks[4], (C,), jnp.float32)
        mu_k = jax.random.uniform(ks[5], (C,), jnp.float32)
        return {'x': x, 'W_r': W_r, 'W_k': W_k, 'W_v': W_v, 'mu_r': mu_r, 'mu_k': mu_k}
    _L0_ffn_in = _L0_ffn_setup()
    _L0_c = _w((lambda *s: np.random.randn(*s).astype(np.float32) * 0.05)(8, 128))
    _L0_wmod = _w((lambda *s: np.random.randn(*s).astype(np.float32) * 0.05)(128, 6 * 128) * 128 ** (-0.5))

    def _L1_attn_setup():
        import jax, jax.numpy as jnp
        import numpy as np
        import math
        DIM = 128
        HEADS = 16
        HEAD_DIM = DIM // HEADS
        key = jax.random.key(seed)
        ks = jax.random.split(key, 7)
        b, n = (2, 256)
        scale = 1.0 / math.sqrt(DIM)
        x = jax.random.normal(ks[0], (b, n, DIM), dtype=jnp.float32)
        Wq = jax.random.normal(ks[1], (DIM, DIM), dtype=jnp.float32) * scale
        Wk = jax.random.normal(ks[2], (DIM, DIM), dtype=jnp.float32) * scale
        Wv = jax.random.normal(ks[3], (DIM, DIM), dtype=jnp.float32) * scale
        Wo = jax.random.normal(ks[4], (DIM, DIM), dtype=jnp.float32) * scale
        bo = jnp.zeros((DIM,), dtype=jnp.float32)
        denom_bias = jnp.zeros((1, HEADS, 1, 1), dtype=jnp.float32)
        return {'x': x, 'Wq': Wq, 'Wk': Wk, 'Wv': Wv, 'Wo': Wo, 'bo': bo, 'denom_bias': denom_bias}
    _L1_attn_in = _L1_attn_setup()

    def _L1_ffn_setup():
        import jax, jax.numpy as jnp
        import numpy as np
        DIM = 128

        def _reference_tuple_inner(x, W_r, W_k, W_v, mu_r, mu_k):
            B, T, C = x.shape
            x_prev = jnp.concatenate([jnp.zeros((B, 1, C), x.dtype), x[:, :-1, :]], axis=1)
            xr = mu_r * x + (1.0 - mu_r) * x_prev
            xk = mu_k * x + (1.0 - mu_k) * x_prev
            r = jax.nn.sigmoid(jnp.einsum('btc,dc->btd', xr, W_r))
            k = jnp.einsum('btc,dc->btd', xk, W_k)
            k_act = jnp.square(jax.nn.relu(k))
            out = r * jnp.einsum('btc,dc->btd', k_act, W_v)
            new_state = x[:, -1, :]
            return (out, new_state)
        key = jax.random.key(seed)
        ks = jax.random.split(key, 6)
        B, T, C = (8, 256, DIM)
        x = jax.random.normal(ks[0], (B, T, C), dtype=jnp.float32)
        s = 1.0 / np.sqrt(C)
        W_r = jax.random.uniform(ks[1], (C, C), jnp.float32, -s, s)
        W_k = jax.random.uniform(ks[2], (C, C), jnp.float32, -s, s)
        W_v = jax.random.uniform(ks[3], (C, C), jnp.float32, -s, s)
        mu_r = jax.random.uniform(ks[4], (C,), jnp.float32)
        mu_k = jax.random.uniform(ks[5], (C,), jnp.float32)
        return {'x': x, 'W_r': W_r, 'W_k': W_k, 'W_v': W_v, 'mu_r': mu_r, 'mu_k': mu_k}
    _L1_ffn_in = _L1_ffn_setup()
    _L1_c = _w((lambda *s: np.random.randn(*s).astype(np.float32) * 0.05)(8, 128))
    _L1_wmod = _w((lambda *s: np.random.randn(*s).astype(np.float32) * 0.05)(128, 6 * 128) * 128 ** (-0.5))
    _d = {'L0_attn_x': _L0_attn_in['x'], 'L0_attn_w_norm': _L0_attn_in['w_norm'], 'L0_attn_W_in': _L0_attn_in['W_in'], 'L0_attn_b_in': _L0_attn_in['b_in'], 'L0_attn_W_x': _L0_attn_in['W_x'], 'L0_attn_b_x': _L0_attn_in['b_x'], 'L0_attn_W_dt': _L0_attn_in['W_dt'], 'L0_attn_b_dt': _L0_attn_in['b_dt'], 'L0_attn_W_out': _L0_attn_in['W_out'], 'L0_attn_b_out': _L0_attn_in['b_out'], 'L0_ffn_W_r': _L0_ffn_in['W_r'], 'L0_ffn_W_k': _L0_ffn_in['W_k'], 'L0_ffn_W_v': _L0_ffn_in['W_v'], 'L0_ffn_mu_r': _L0_ffn_in['mu_r'], 'L0_ffn_mu_k': _L0_ffn_in['mu_k'], 'L0_c': _L0_c, 'L0_wmod': _L0_wmod, 'L1_attn_Wq': _L1_attn_in['Wq'], 'L1_attn_Wk': _L1_attn_in['Wk'], 'L1_attn_Wv': _L1_attn_in['Wv'], 'L1_attn_Wo': _L1_attn_in['Wo'], 'L1_attn_bo': _L1_attn_in['bo'], 'L1_attn_denom_bias': _L1_attn_in['denom_bias'], 'L1_ffn_W_r': _L1_ffn_in['W_r'], 'L1_ffn_W_k': _L1_ffn_in['W_k'], 'L1_ffn_W_v': _L1_ffn_in['W_v'], 'L1_ffn_mu_r': _L1_ffn_in['mu_r'], 'L1_ffn_mu_k': _L1_ffn_in['mu_k'], 'L1_c': _L1_c, 'L1_wmod': _L1_wmod}
    _x0 = _d['L0_attn_x']
    _d['L0_attn_x'] = jax.random.normal(jax.random.fold_in(jax.random.key(seed), 1), (8, 512, 128), dtype=_x0.dtype)
    del _x0
    return _d

def reference(L0_attn_x, L0_attn_w_norm, L0_attn_W_in, L0_attn_b_in, L0_attn_W_x, L0_attn_b_x, L0_attn_W_dt, L0_attn_b_dt, L0_attn_W_out, L0_attn_b_out, L0_ffn_W_r, L0_ffn_W_k, L0_ffn_W_v, L0_ffn_mu_r, L0_ffn_mu_k, L0_c, L0_wmod, L1_attn_Wq, L1_attn_Wk, L1_attn_Wv, L1_attn_Wo, L1_attn_bo, L1_attn_denom_bias, L1_ffn_W_r, L1_ffn_W_k, L1_ffn_W_v, L1_ffn_mu_r, L1_ffn_mu_k, L1_c, L1_wmod):

    def _L0_attn_ref(x, w_norm, W_in, b_in, W_x, b_x, W_dt, b_dt, W_out, b_out):
        import jax, jax.numpy as jnp
        import numpy as np
        EPS = 1e-08

        def rmsnorm(x, w):
            norm = jax.lax.rsqrt(jnp.mean(x * x, axis=-1, keepdims=True) + EPS)
            return x * norm * w
        residual = x
        xn = rmsnorm(x, w_norm)
        uzg = xn @ W_in + b_in
        S = uzg.shape[-1] // 3
        u, z, g = (uzg[..., :S], uzg[..., S:2 * S], uzg[..., 2 * S:])
        ut = jnp.tanh(u @ W_x + b_x)
        dt = jax.nn.sigmoid(z @ W_dt + b_dt)

        def step(h, inp):
            u_t, dt_t = inp
            h = (1.0 - dt_t) * h + dt_t * u_t
            return (h, h)
        h0 = jnp.zeros(ut.shape[::2][::-1][:0] + (ut.shape[0], ut.shape[2]), ut.dtype)
        _, hs = jax.lax.scan(step, h0, (ut.transpose(1, 0, 2), dt.transpose(1, 0, 2)))
        hs = hs.transpose(1, 0, 2)
        y = hs * jax.nn.sigmoid(g)
        y = y @ W_out + b_out
        return residual + y

    def _L0_ffn_ref(x, W_r, W_k, W_v, mu_r, mu_k):
        import jax, jax.numpy as jnp
        import numpy as np
        DIM = 128

        def _reference_tuple_inner(x, W_r, W_k, W_v, mu_r, mu_k):
            B, T, C = x.shape
            x_prev = jnp.concatenate([jnp.zeros((B, 1, C), x.dtype), x[:, :-1, :]], axis=1)
            xr = mu_r * x + (1.0 - mu_r) * x_prev
            xk = mu_k * x + (1.0 - mu_k) * x_prev
            r = jax.nn.sigmoid(jnp.einsum('btc,dc->btd', xr, W_r))
            k = jnp.einsum('btc,dc->btd', xk, W_k)
            k_act = jnp.square(jax.nn.relu(k))
            out = r * jnp.einsum('btc,dc->btd', k_act, W_v)
            new_state = x[:, -1, :]
            return (out, new_state)
        return _reference_tuple_inner(x, W_r, W_k, W_v, mu_r, mu_k)[0]

    def _L1_attn_ref(x, Wq, Wk, Wv, Wo, bo, denom_bias):
        import jax, jax.numpy as jnp
        import numpy as np
        import math
        DIM = 128
        HEADS = 16
        HEAD_DIM = DIM // HEADS
        b, n, d = x.shape
        h, hd = (HEADS, HEAD_DIM)

        def split_heads(t):
            return t.reshape(b, n, h, hd).transpose(0, 2, 1, 3)
        q = split_heads(x @ Wq.T)
        k = split_heads(x @ Wk.T)
        v = split_heads(x @ Wv.T)
        sim = jnp.einsum('bhid,bhjd->bhij', q, k) / math.sqrt(hd)
        causal_mask = jnp.triu(jnp.ones((n, n), dtype=bool), k=1)
        neg = -jnp.finfo(sim.dtype).max
        sim = jnp.where(causal_mask, neg, sim)
        sim_max = jnp.max(sim, axis=-1, keepdims=True)
        exp_sim = jnp.exp(sim - sim_max)
        denom = jnp.sum(exp_sim, axis=-1, keepdims=True) + jnp.exp(denom_bias)
        attn = exp_sim / denom
        out = jnp.einsum('bhij,bhjd->bhid', attn, v)
        out = out.transpose(0, 2, 1, 3).reshape(b, n, d)
        return out @ Wo.T + bo

    def _L1_ffn_ref(x, W_r, W_k, W_v, mu_r, mu_k):
        import jax, jax.numpy as jnp
        import numpy as np
        DIM = 128

        def _reference_tuple_inner(x, W_r, W_k, W_v, mu_r, mu_k):
            B, T, C = x.shape
            x_prev = jnp.concatenate([jnp.zeros((B, 1, C), x.dtype), x[:, :-1, :]], axis=1)
            xr = mu_r * x + (1.0 - mu_r) * x_prev
            xk = mu_k * x + (1.0 - mu_k) * x_prev
            r = jax.nn.sigmoid(jnp.einsum('btc,dc->btd', xr, W_r))
            k = jnp.einsum('btc,dc->btd', xk, W_k)
            k_act = jnp.square(jax.nn.relu(k))
            out = r * jnp.einsum('btc,dc->btd', k_act, W_v)
            new_state = x[:, -1, :]
            return (out, new_state)
        return _reference_tuple_inner(x, W_r, W_k, W_v, mu_r, mu_k)[0]
    x = L0_attn_x
    mod = (_silu(L0_c) @ L0_wmod).reshape(L0_c.shape[0], 6, 1, -1)
    sa, ca, ga, sb, cb, gb = (mod[:, 0], mod[:, 1], mod[:, 2], mod[:, 3], mod[:, 4], mod[:, 5])
    ga = (2 * (ga >= 0) - 1) * jnp.maximum(jnp.abs(ga), 0.25)
    gb = (2 * (gb >= 0) - 1) * jnp.maximum(jnp.abs(gb), 0.25)
    h = _layernorm(x, axis=-1) * (1 + ca) + sa
    x = x + ga * _L0_attn_ref(h, L0_attn_w_norm, L0_attn_W_in, L0_attn_b_in, L0_attn_W_x, L0_attn_b_x, L0_attn_W_dt, L0_attn_b_dt, L0_attn_W_out, L0_attn_b_out)
    h = _layernorm(x, axis=-1) * (1 + cb) + sb
    x = x + gb * _L0_ffn_ref(h, L0_ffn_W_r, L0_ffn_W_k, L0_ffn_W_v, L0_ffn_mu_r, L0_ffn_mu_k)
    mod = (_silu(L1_c) @ L1_wmod).reshape(L1_c.shape[0], 6, 1, -1)
    sa, ca, ga, sb, cb, gb = (mod[:, 0], mod[:, 1], mod[:, 2], mod[:, 3], mod[:, 4], mod[:, 5])
    ga = (2 * (ga >= 0) - 1) * jnp.maximum(jnp.abs(ga), 0.25)
    gb = (2 * (gb >= 0) - 1) * jnp.maximum(jnp.abs(gb), 0.25)
    h = _layernorm(x, axis=-1) * (1 + ca) + sa
    x = x + ga * _L1_attn_ref(h, L1_attn_Wq, L1_attn_Wk, L1_attn_Wv, L1_attn_Wo, L1_attn_bo, L1_attn_denom_bias)
    h = _layernorm(x, axis=-1) * (1 + cb) + sb
    x = x + gb * _L1_ffn_ref(h, L1_ffn_W_r, L1_ffn_W_k, L1_ffn_W_v, L1_ffn_mu_r, L1_ffn_mu_k)
    return x

_drawn_inputs = setup_inputs


def setup_inputs(seed=0):
    import zlib

    import numpy as np

    out = dict(_drawn_inputs(seed))
    spreads = {'L0_attn_w_norm': (1.0, 0.6),
     'L0_attn_b_in': (0.0, 0.8),
     'L0_attn_b_x': (0.0, 0.8),
     'L0_attn_b_dt': (0.0, 0.8),
     'L0_attn_b_out': (0.0, 0.338),
     'L1_attn_bo': (0.0, 2.0),
     'L1_attn_denom_bias': (0.0, 2.0)}
    factors = {'L0_ffn_W_r': 8.0,
     'L0_ffn_W_k': 3.052,
     'L0_ffn_W_v': 2.808,
     'L0_ffn_mu_r': 8.0,
     'L0_ffn_mu_k': 4.745,
     'L1_ffn_W_r': 8.0,
     'L1_ffn_W_k': 3.054,
     'L1_ffn_W_v': 2.829,
     'L1_ffn_mu_r': 8.0,
     'L1_ffn_mu_k': 4.754,
     'L1_attn_Wq': 8.0,
     'L1_attn_Wk': 8.0,
     'L1_attn_Wv': 7.947,
     'L1_attn_Wo': 7.968}
    for name, (base, spread) in spreads.items():
        noise = np.random.default_rng([zlib.crc32(name.encode()), seed]).standard_normal(out[name].shape)
        drawn = base * np.exp(spread * noise) if base else spread * noise
        out[name] = jnp.asarray(drawn.astype(out[name].dtype))
    for name, factor in factors.items():
        out[name] = (out[name] * factor).astype(out[name].dtype)
    return out
```

```python
from contextlib import ExitStack

import concourse.bass as bass
from concourse import mybir

ALU = mybir.AluOpType
ACT = mybir.ActivationFunctionType
AX_X = mybir.AxisListType.X
F32 = mybir.dt.float32
BF16 = mybir.dt.bfloat16

NB = 8
L = 512
D = 128
P = 128
NT = L // P
S = 32
H = 16
HD = D // H
HG = 4
NG = H // HG
NU = 10
HALF = 64
PARTS = 3
Q_SLOT = (0, 1, 2, 0, 1, 0)
K_SLOT = (0, 0, 0, 1, 1, 2)
NS = len(Q_SLOT)
KA = NS * HD
KB = KA + PARTS
NEG = -1.0e30
LN_EPS = 1e-5
RMS_EPS = 1e-8
LOADS = 2 * 2 * NS
EXP_BANK = (0, 1, 2, 0, 1, 2, 0, 1, 2, 1)
EXP_BACK = (4, 2, 4, 3, 3, 3, 3, 3, 3, 2)


def build(nc, x, w_in, w_norm, b_in, w_x, b_x, w_dt, b_dt, w_out, b_out, f0, c0T, wmod0,
          wqT, wkT, wvT, woT, bo, denom_bias, f1, c1T, wmod1, out):
    ctx = ExitStack()
    with ctx:
        def sb(name, shape, dt=F32):
            return ctx.enter_context(nc.sbuf_tensor(name, shape, dt))

        def bank(name):
            return ctx.enter_context(nc.psum_tensor(name, [P, 512], F32))

        def sem(name):
            return ctx.enter_context(nc.semaphore(name))

        mod_dram = nc.dram_tensor("mod_rows", (NB, 6 * D), F32).ap()
        q_dram = nc.dram_tensor("q_parts", (2, PARTS, H, HD, L), BF16).ap()
        k_dram = nc.dram_tensor("k_parts", (2, PARTS, H, HD, L), BF16).ap()

        ident = sb("ident", [P, P])
        identb = sb("identb", [P, P], BF16)
        mask_q = sb("mask_q", [P, 2, P], BF16)
        mask_k = sb("mask_k", [P, 2, P], BF16)
        neg_half = sb("neg_half", [P, NT])
        w_in_sb = sb("w_in_sb", [P, 3 * S])
        w_norm_sb = sb("w_norm_sb", [P, 1])
        b_uz = sb("b_uz", [2 * S, 1])
        b_g = sb("b_g", [S, 1])
        w_xdt = sb("w_xdt", [2 * S, S])
        b_x_sb = sb("b_x_sb", [S, 1])
        b_dt_sb = sb("b_dt_sb", [S, 1])
        w_out_sb = sb("w_out_sb", [S + 1, D])
        c_sb = sb("c_sb", [P, 2, NB])
        c_tanh = sb("c_tanh", [P, 2, NB])
        c_silu = sb("c_silu", [P, 2, NB])
        wmod_sb = sb("wmod_sb", [P, 2, 6 * D])
        mod_col = sb("mod_col", [P, 6, NB])
        mod_row = sb("mod_row", [NB, 6, D])
        wq_sb = sb("wq_sb", [P, D])
        wk_sb = sb("wk_sb", [P, D])
        wv_sb = sb("wv_sb", [P, D])
        wo_sb = sb("wo_sb", [P, D])
        bo_sb = sb("bo_sb", [P, D])
        exp_bias = sb("exp_bias", [P, H])
        ffn_w = sb("ffn_w", [P, 2, 3, D])
        ffn_mu = sb("ffn_mu", [P, 2, 2])
        ffn_now = sb("ffn_now", [P, 2, 2, D])
        ffn_prev = sb("ffn_prev", [P, 2, 2, D])

        mod = sb("mod", [P, 2, 6, D])
        x_in = sb("x_in", [P, 2, NT, D])
        stats = [sb(f"stats{n}", [P, NT, 6]) for n in range(4)]
        mean_var = [sb(f"mean_var{n}", [P, NT, 2]) for n in range(4)]
        var_eps = [sb(f"var_eps{n}", [P, NT]) for n in range(4)]
        rstd = [sb(f"rstd{n}", [P, NT]) for n in range(4)]
        x_hat = [sb(f"x_hat{n}", [P, NT, D]) for n in range(4)]
        h_scaled = x_hat[0]
        h_tok = sb("h_tok", [P, NT, D])
        h_sq = sb("h_sq", [P, NT, D])
        h_sum = sb("h_sum", [P, NT])
        h_mean = sb("h_mean", [P, NT])
        h_rms = sb("h_rms", [P, NT])
        h_norm = h_sq
        hn_ch = sb("hn_ch", [P, L])
        gate_h = x_hat[0]
        x_plus_h = x_hat[0]
        w_out_g = sb("w_out_g", [S + 1, D])
        g_tanh = sb("g_tanh", [S, L])
        uz = sb("uz", [2 * S, L])
        u_tanh = sb("u_tanh", [S, L])
        dt_tanh = sb("dt_tanh", [S, L])
        keep = sb("keep", [S, L])
        feed = sb("feed", [S, L])
        state = sb("state", [S, L])
        y = sb("y", [S + 1, L])
        gate_raw, gate_sign, gate_abs, gate_size = (t[0:NB, :].rearrange("b (k c) -> b k c", k=4)
                                          for t in (keep, feed, state, u_tanh))
        x1 = sb("x1", [P, NT, D])
        x2 = sb("x2", [P, NT, D])
        x_bo = sb("x_bo", [P, 2, NT, D])
        g_bo = sb("g_bo", [P, D])
        x3 = sb("x3", [P, NT, D])
        x4 = sb("x4", [P, NT, D])
        wo_g = sb("wo_g", [P, 2, D])
        wv_g = [sb("wv_g0", [P, 1, D]), sb("wv_g1", [P, 2, D])]
        h_ch = [sb(f"h_ch{n}", [P, 1 + L]) for n in range(3)]
        r_tanh = [sb(f"r_tanh{n}", [P, L]) for n in range(2)]
        k_relu = [sb(f"k_relu{n}", [P, L]) for n in range(2)]
        k_sq = k_relu
        ffn_out = [sb(f"ffn_out{n}", [P, NT, D]) for n in range(2)]
        qk_full = sb("qk_full", [P, 2, L])
        qk_rest = sb("qk_rest", [P, 2, L])
        qk_part = sb("qk_part", [P, 2, PARTS, L], BF16)
        q_stack = sb("q_stack", [P, 2, H // 2, L], BF16)
        k_stack = sb("k_stack", [P, 2, H // 2, L], BF16)
        v_aug = sb("v_aug", [P, 2, NT, H, 32])
        neg_max = sb("neg_max", [P, 2, HG, NT])
        max_rest = sb("max_rest", [P, HG, NT])
        max_part = sb("max_part", [P, HG, PARTS, NT], BF16)
        max_rows = sb("max_rows", [HG * PARTS * NT, 2, P], BF16)
        probs = sb("probs", [P, 2, NU, 512])
        o_heads = sb("o_heads", [P, L])
        denom = sb("denom", [P, NT, HG])
        denom_inv = sb("denom_inv", [P, NT, HG])
        o_tok = sb("o_tok", [P, NT, D])
        o_ch = sb("o_ch", [P, L])

        row_bank = [bank(f"row_bank{n}") for n in range(2)]
        col_bank = [bank(f"col_bank{n}") for n in range(3)]
        pv_bank = bank("pv_bank")
        misc = bank("misc")
        turn = bank("turn")
        turn_b = turn[:, :].bitcast(BF16)

        names = """w_loaded pool_const vec_const y_ones c_tanh_done c_silu_done modrow_ps modcol_ps
        mod_ready gate_step modrow_done mod_stored ffn_w_done act_const pool_step
        mod_loaded x_loaded xin_free
        ln0_stat ln0_mv ln0_rs ln1_stat ln1_mv ln1_rs ln2_stat ln2_mv ln2_rs ln3_stat ln3_mv ln3_rs
        ln1_xhat ln2_xhat ln3_xhat ln0_xhat
        h_step h_done h_sq_done h_sum_done rms_step hn_done xh_done wog_done
        hn_ps hn_copied g_ps g_done uz_ps uz_done ut_ps ut_done dt_ps dt_done
        scan_step y_done out_ps x1_done
        hc0_ps hc0_done r0_ps r0_done k0_ps k0_done ksq0_done kv0_ps kv0_done x2_done
        hc1_ps hc1_done q_ps q_done k_ps k_done v_ps v_done
        split_q1 split_r1 split_q2 split_q3 parts_stored stacks_loaded xbo_done wg0_done wg1_done gbo_done gateh_done
        row_ready row_read max_ready max_step max_split max_ps max_copied max_loaded
        col_ready exp_done pv_done o_copied turn_ready denom_step o_norm
        oc_ps oc_done wo_ps x3_done hc2_ps hc2_done r1_ps r1_done k1_ps k1_done ksq1_done kv1_ps kv1_done
        x4_done out_stored waited""".split()
        s = {name: sem(name) for name in names}

        def floor0(count):
            return max(count, 0) if isinstance(count, int) else count

        def stand_alone(eng, count):
            if not isinstance(count, int):
                eng.sem_inc(s["waited"], 1)

        def over(t):
            return t.unsqueeze(1).broadcast_to([t.shape[0], NT, t.shape[1]])

        def along(t):
            return t.unsqueeze(2).broadcast_to([P, NT, D])

        def tiles(t):
            return t.rearrange("p (t c) -> p t c", t=NT)

        def real(b):
            return not isinstance(b, int) or 0 <= b < NB

        def iterations(eng, body):
            body(-1, 1)
            body(0, 0)
            with eng.Fori(1, NB - 2, 2) as i:
                body(i, 1)
                body(i + 1, 0)
            body(NB - 1, 1)
            body(NB, 0)

        def group(i, step, back):
            g = step - back
            if g >= 0:
                return i, 0, g, NG * i + g
            return i - 1, 1, g + NG, NG * i + g

        block = ctx.enter_context(nc.Block())

        @block.sync
        def _(sp):
            def load(dst, src, name):
                sp.dma_start(dst, src).then_inc(s[name], 16)

            def col(v, lo, hi):
                return v[lo:hi].rearrange("(p o) -> p o", o=1)

            def load_x(b, p):
                load(x_in[:, p], x[bass.ds(b, 1)].rearrange("o (t p) c -> p (o t) c", p=P), "x_loaded")

            def load_mod(b, p):
                row = mod_dram[bass.ds(b, 1), :].rearrange("o n -> (o n)").partition_broadcast(P)
                load(mod[:, p].rearrange("p k c -> p (k c)"), row, "mod_loaded")

            sp.sem_inc(s["out_stored"], 16)
            load(c_sb[:, 0], c0T, "w_loaded")
            load(c_sb[:, 1], c1T, "w_loaded")
            load(wmod_sb[:, 0], wmod0, "w_loaded")
            load(wmod_sb[:, 1], wmod1, "w_loaded")
            load_x(0, 0)
            load(w_in_sb[:, :], w_in, "w_loaded")
            load(w_norm_sb[:, :], col(w_norm, 0, D), "w_loaded")
            load(b_uz[:, :], col(b_in, 0, 2 * S), "w_loaded")
            load(b_g[:, :], col(b_in, 2 * S, 3 * S), "w_loaded")
            load(w_xdt[0:S, :], w_x, "w_loaded")
            load(w_xdt[S:2 * S, :], w_dt, "w_loaded")
            load(b_x_sb[:, :], col(b_x, 0, S), "w_loaded")
            load(b_dt_sb[:, :], col(b_dt, 0, S), "w_loaded")
            load(w_out_sb[0:S, :], w_out, "w_loaded")
            load(w_out_sb[S:S + 1, :], b_out.rearrange("(o n) -> o n", o=1), "w_loaded")
            for dst, src in ((wq_sb, wqT), (wk_sb, wkT), (wv_sb, wvT), (wo_sb, woT)):
                load(dst[:, :], src, "w_loaded")
            load(bo_sb[:, :], bo.partition_broadcast(P), "w_loaded")
            load(exp_bias[:, :], denom_bias.rearrange("a h b c -> (a h b c)").partition_broadcast(P), "w_loaded")
            for n, f in enumerate((f0, f1)):
                for j in range(3):
                    load(ffn_w[:, n, j], f[j], "w_loaded")
                for j in range(2):
                    load(ffn_mu[:, n, j:j + 1], col(f[3 + j], 0, D), "w_loaded")
            sp.wait_ge(s["modrow_done"], 2)
            stand_alone(sp, 2)
            load(mod_dram.rearrange("b (k c) -> b k c", k=6), mod_row[:, :, :], "mod_stored")
            sp.wait_ge(s["mod_stored"], 16)
            stand_alone(sp, 16)
            sp.wait_ge(s["pool_const"], 7)
            stand_alone(sp, 7)

            def max_load(G, par, g, gp):
                sp.wait_ge(s["max_copied"], G + 1)
                stand_alone(sp, G + 1)
                for k in range(HG):
                    t, half = 2 * g + k // 2, k % 2
                    load(q_stack[HALF * half + KA:HALF * half + KB, par, t, :],
                         max_rows[12 * k:12 * k + 12, gp, :], "max_loaded")

            def body(i, p):
                fb = i + 1
                if real(fb):
                    sp.wait_ge(s["xbo_done"], floor0(i))
                    stand_alone(sp, i)
                    sp.wait_ge(s["wg1_done"], floor0(2 * i))
                    stand_alone(sp, i)
                    if not isinstance(i, int) or i >= 0:
                        sp.wait_ge(s["xh_done"], i)
                        stand_alone(sp, i)
                        load_x(fb, 1 - p)
                    load_mod(fb, 1 - p)
                for st in range(NG):
                    b, dp, g, G = group(i, st, 1)
                    if real(b):
                        max_load(G, (p + dp) % 2, g, g % 2)
                if real(fb):
                    q = 1 - p
                    sp.wait_ge(s["split_q3"], 2 * (fb + 1))
                    stand_alone(sp, 2 * (fb + 1))
                    sp.wait_ge(s["split_q2"], 2 * (fb + 1))
                    stand_alone(sp, 2 * (fb + 1))
                    sp.wait_ge(s["split_q1"], 2 * (fb + 1))
                    stand_alone(sp, 2 * (fb + 1))
                    for n, dram in enumerate((q_dram, k_dram)):
                        load(dram[q].rearrange("j h d l -> (h d) j l"), qk_part[:, n], "parts_stored")
                    sp.wait_ge(s["parts_stored"], 32 * (fb + 1))
                    stand_alone(sp, 32 * (fb + 1))
                    sp.wait_ge(s["col_ready"], floor0(NU * NG * (fb - 1)))
                    stand_alone(sp, NU * NG * (fb - 1))
                    for stack, dram, slots in ((q_stack, q_dram, Q_SLOT), (k_stack, k_dram, K_SLOT)):
                        for half in range(2):
                            for j, part in enumerate(slots):
                                row = HALF * half + HD * j
                                src = dram[q, part].rearrange("(t s) d l -> s d t l", s=2)[half]
                                load(stack[row:row + HD, q], src, "stacks_loaded")
                if real(i - 1):
                    sp.wait_ge(s["x4_done"], i)
                    stand_alone(sp, i)
                    dst = out[bass.ds(i - 1, 1)].rearrange("o (t p) c -> p (o t) c", p=P)
                    load(dst, x4[:, :, :], "out_stored")

            iterations(sp, body)
            sp.wait_ge(s["out_stored"], 16 * (NB + 1))
            stand_alone(sp, 16 * (NB + 1))

        @block.gpsimd
        def _(pool):
            nc.gpsimd.memset(ident[:, :], 0.0).then_inc(s["pool_step"], 1)
            nc.gpsimd.memset(identb[:, :], 0.0).then_inc(s["pool_step"], 1)
            nc.gpsimd.memset(mask_q[:, :, :], 0.0).then_inc(s["pool_step"], 1)
            nc.gpsimd.memset(mask_k[:, :, :], 0.0).then_inc(s["pool_step"], 1)
            pool.wait_ge(s["pool_step"], 4)
            stand_alone(pool, 4)
            for m in (ident, identb):
                nc.gpsimd.affine_select(m[:, :], m[:, :], [[-1, P]], ALU.not_equal, 1.0, base=0,
                                        channel_multiplier=1).then_inc(s["pool_const"], 1)
            nc.gpsimd.affine_select(mask_q[:, :, :], mask_q[:, :, :], [[0, 2], [-1, P]], ALU.is_ge, NEG,
                                    base=0, channel_multiplier=1).then_inc(s["pool_const"], 1)
            nc.gpsimd.affine_select(mask_k[:, :, :], mask_k[:, :, :], [[0, 2], [1, P]], ALU.is_ge, NEG,
                                    base=0, channel_multiplier=-1).then_inc(s["pool_const"], 1)
            nc.gpsimd.memset(neg_half[:, :], -0.5).then_inc(s["pool_const"], 1)
            nc.gpsimd.memset(k_stack[:, 0], 1.0).then_inc(s["pool_const"], 1)
            nc.gpsimd.memset(k_stack[:, 1], 1.0).then_inc(s["pool_const"], 1)
            pool.wait_ge(s["pool_const"], 7)
            stand_alone(pool, 7)

            def inv_std(n, b):
                pool.wait_ge(s[f"ln{n}_mv"], NT * (b + 1))
                stand_alone(pool, NT * (b + 1))
                nc.gpsimd.tensor_scalar(var_eps[n][:, :], mean_var[n][:, :, 1], LN_EPS, None,
                                        ALU.add).then_inc(s[f"ln{n}_rs"], 1)
                pool.wait_ge(s[f"ln{n}_rs"], 2 * b + 1)
                stand_alone(pool, 2 * b + 1)
                nc.gpsimd.tensor_tensor(rstd[n][:, :], var_eps[n][:, :], neg_half[:, :],
                                        ALU.pow).then_inc(s[f"ln{n}_rs"], 1)
                pool.wait_ge(s[f"ln{n}_rs"], 2 * b + 2)
                stand_alone(pool, 2 * b + 2)

            def normalize(n, b, src):
                inv_std(n, b)
                for t in range(NT):
                    nc.gpsimd.tensor_scalar(x_hat[n][:, t], src[:, t], mean_var[n][:, t, 0:1],
                                            rstd[n][:, t:t + 1], ALU.subtract,
                                            ALU.mult).then_inc(s[f"ln{n}_xhat"], 1)

            def front_h(b, q):
                pool.wait_ge(s["x_loaded"], 16 * (b + 1))
                stand_alone(pool, 16 * (b + 1))
                normalize(0, b, x_in[:, q])
                pool.wait_ge(s["ln0_xhat"], NT * (b + 1))
                stand_alone(pool, NT * (b + 1))
                pool.wait_ge(s["mod_loaded"], 16 * (b + 1))
                stand_alone(pool, 16 * (b + 1))
                nc.gpsimd.tensor_tensor(h_scaled[:, :, :], x_hat[0][:, :, :], over(mod[:, q, 1]),
                                        ALU.mult).then_inc(s["h_step"], 1)
                pool.wait_ge(s["h_step"], b + 1)
                stand_alone(pool, b + 1)
                nc.gpsimd.tensor_tensor(h_tok[:, :, :], h_scaled[:, :, :], over(mod[:, q, 0]),
                                        ALU.add).then_inc(s["h_done"], 1)
                pool.wait_ge(s["h_done"], b + 1)
                stand_alone(pool, b + 1)

            def front_rms(b):
                pool.wait_ge(s["h_sum_done"], b + 1)
                stand_alone(pool, b + 1)
                nc.gpsimd.tensor_scalar(h_mean[:, :], h_sum[:, :], 1.0 / D, RMS_EPS, ALU.mult,
                                        ALU.add).then_inc(s["rms_step"], 1)
                pool.wait_ge(s["rms_step"], 2 * b + 1)
                stand_alone(pool, 2 * b + 1)
                nc.gpsimd.tensor_tensor(h_rms[:, :], h_mean[:, :], neg_half[:, :],
                                        ALU.pow).then_inc(s["rms_step"], 1)
                pool.wait_ge(s["rms_step"], 2 * b + 2)
                stand_alone(pool, 2 * b + 2)
                nc.gpsimd.tensor_tensor(h_norm[:, :, :], h_tok[:, :, :], along(h_rms[:, :]),
                                        ALU.mult).then_inc(s["hn_done"], 1)

            def front_xh(b, q):
                nc.gpsimd.tensor_tensor(gate_h[:, :, :], h_tok[:, :, :], over(mod[:, q, 2]),
                                        ALU.mult).then_inc(s["gateh_done"], 1)
                pool.wait_ge(s["gateh_done"], b + 1)
                stand_alone(pool, b + 1)
                nc.gpsimd.tensor_tensor(x_plus_h[:, :, :], gate_h[:, :, :], x_in[:, q],
                                        ALU.add).then_inc(s["xh_done"], 1)
                nc.gpsimd.tensor_tensor(w_out_g[:, :], w_out_sb[:, :], mod[0:S + 1, q, 2],
                                        ALU.mult).then_inc(s["wog_done"], 1)
                nc.gpsimd.tensor_tensor(wv_g[0][:, 0], ffn_w[:, 0, 2], mod[:, q, 3],
                                        ALU.mult).then_inc(s["wg0_done"], 1)

            def square(n, b):
                pool.wait_ge(s[f"k{n}_done"], b + 1)
                stand_alone(pool, b + 1)
                nc.gpsimd.tensor_tensor(k_sq[n][:, :], k_relu[n][:, :], k_relu[n][:, :],
                                        ALU.mult).then_inc(s[f"ksq{n}_done"], 1)

            def residual(dst, src, n, b, done):
                pool.wait_ge(s[f"kv{n}_done"], b + 1)
                stand_alone(pool, b + 1)
                nc.gpsimd.tensor_tensor(dst[:, :, :], src[:, :, :], ffn_out[n][:, :, :],
                                        ALU.add).then_inc(s[done], 1)

            def rest(n, b):
                pool.wait_ge(s["split_q1"], 2 * b + n + 1)
                stand_alone(pool, 2 * b + n + 1)
                nc.gpsimd.tensor_tensor(qk_rest[:, n], qk_full[:, n], qk_part[:, n, 0],
                                        ALU.subtract).then_inc(s["split_r1"], 1)

            def last_part(n, b):
                pool.wait_ge(s["split_q2"], 2 * b + n + 1)
                stand_alone(pool, 2 * b + n + 1)
                nc.gpsimd.tensor_tensor(qk_part[:, n, 2], qk_rest[:, n], qk_part[:, n, 1],
                                        ALU.subtract).then_inc(s["split_q3"], 1)

            def max_parts(G, gp):
                pool.wait_ge(s["max_ready"], G + 1)
                stand_alone(pool, G + 1)
                if not isinstance(G, int) or G > 0:
                    pool.wait_ge(s["max_ps"], G)
                    stand_alone(pool, G)
                full = neg_max[:, gp]
                nc.gpsimd.tensor_copy(max_part[:, :, 0, :], full).then_inc(s["max_step"], 1)
                pool.wait_ge(s["max_step"], 3 * G + 1)
                stand_alone(pool, 3 * G + 1)
                nc.gpsimd.tensor_tensor(max_rest[:, :, :], full, max_part[:, :, 0, :],
                                        ALU.subtract).then_inc(s["max_step"], 1)
                pool.wait_ge(s["max_step"], 3 * G + 2)
                stand_alone(pool, 3 * G + 2)
                nc.gpsimd.tensor_copy(max_part[:, :, 1, :], max_rest[:, :, :]).then_inc(s["max_step"], 1)
                pool.wait_ge(s["max_step"], 3 * G + 3)
                stand_alone(pool, 3 * G + 3)
                nc.gpsimd.tensor_tensor(max_part[:, :, 2, :], max_rest[:, :, :], max_part[:, :, 1, :],
                                        ALU.subtract).then_inc(s["max_split"], 1)

            def xbo(b, p):
                pool.wait_ge(s["x2_done"], b + 1)
                stand_alone(pool, b + 1)
                nc.gpsimd.tensor_tensor(g_bo[:, :], bo_sb[:, :], mod[:, p, 4], ALU.mult)\
                    .then_inc(s["gbo_done"], 1)
                pool.wait_ge(s["gbo_done"], b + 1)
                stand_alone(pool, b + 1)
                nc.gpsimd.tensor_tensor(x_bo[:, p], x2[:, :, :], over(g_bo[:, :]),
                                        ALU.add).then_inc(s["xbo_done"], 1)
                nc.gpsimd.tensor_tensor(wo_g[:, p], wo_sb[:, :], mod[:, p, 4],
                                        ALU.mult).then_inc(s["wg1_done"], 1)
                nc.gpsimd.tensor_tensor(wv_g[1][:, p], ffn_w[:, 1, 2], mod[:, p, 5],
                                        ALU.mult).then_inc(s["wg1_done"], 1)

            pool.wait_ge(s["vec_const"], 1)
            stand_alone(pool, 1)
            pool.wait_ge(s["act_const"], 1)
            stand_alone(pool, 1)

            def body(i, p):
                b, q = i + 1, 1 - p
                for st in range(NG):
                    mb, _, g, G = group(i, st, 1)
                    if real(mb):
                        max_parts(G, g % 2)
                    if st == 0 and real(b):
                        front_h(b, q)
                        front_rms(b)
                    if st == 0 and real(i):
                        xbo(i, p)
                    if st == 1 and real(b):
                        front_xh(b, q)
                        pool.wait_ge(s["x1_done"], b + 1)
                        stand_alone(pool, b + 1)
                        normalize(1, b, x1)
                    if st == 2 and real(b):
                        square(0, b)
                        residual(x2, x1, 0, b, "x2_done")
                        normalize(2, b, x2)
                        rest(0, b)
                        rest(1, b)
                        last_part(0, b)
                        last_part(1, b)
                    if st == 3 and real(i - 1):
                        pool.wait_ge(s["x3_done"], i)
                        stand_alone(pool, i)
                        normalize(3, i - 1, x3)
                        square(1, i - 1)
                        pool.wait_ge(s["out_stored"], 16 * i)
                        stand_alone(pool, 16 * i)
                        residual(x4, x3, 1, i - 1, "x4_done")

            iterations(pool, body)

        @block.scalar
        def _(act):
            act.wait_ge(s["w_loaded"], 16 * N_WEIGHTS)
            nc.scalar.activation(c_tanh[:, :, :], c_sb[:, :, :], ACT.Tanh, scale=0.5).then_inc(s["c_tanh_done"], 1)
            nc.scalar.activation(exp_bias[:, :], exp_bias[:, :], ACT.Exp).then_inc(s["act_const"], 1)
            act.wait_ge(s["vec_const"], 1)
            act.wait_ge(s["mod_ready"], 1)

            def to_channels(n, b, k):
                act.wait_ge(s[f"hc{n}_ps"], b + 1)
                nc.scalar.activation(h_ch[n][:, 1:1 + L], misc[:, :], ACT.Identity,
                                     scale=mod_col[:, k, bass.ds(b, 1)],
                                     bias=mod_col[:, k + 3, bass.ds(b, 1)]).then_inc(s[f"hc{n}_done"], 1)

            def ffn_r(n, b):
                act.wait_ge(s[f"r{n}_ps"], b + 1)
                nc.scalar.activation(r_tanh[n][:, :], misc[:, :], ACT.Tanh, scale=0.5)\
                    .then_inc(s[f"r{n}_done"], 1)

            def ffn_k(n, b):
                act.wait_ge(s[f"k{n}_ps"], b + 1)
                nc.scalar.activation(k_relu[n][:, :], misc[:, :], ACT.Relu).then_inc(s[f"k{n}_done"], 1)

            def exps(G, k, gp):
                if k == 0:
                    act.wait_ge(s["pv_done"], floor0(G - 1))
                act.wait_ge(s["col_ready"], NU * G + k + 1)
                nc.scalar.activation(probs[:, gp, k], col_bank[EXP_BANK[k]][:, :], ACT.Exp)\
                    .then_inc(s["exp_done"], 1)

            def front(b, q, at):
                if at == 5:
                    act.wait_ge(s["h_done"], b + 1)
                    nc.scalar.activation(h_sq[:, :, :], h_tok[:, :, :], ACT.Square).then_inc(s["h_sq_done"], 1)
                elif at == 8:
                    act.wait_ge(s["hn_ps"], b + 1)
                    nc.scalar.activation(hn_ch[:, :], misc[:, :], ACT.Copy).then_inc(s["hn_copied"], 1)
                elif at == 9:
                    act.wait_ge(s["g_ps"], b + 1)
                    nc.scalar.activation(g_tanh[:, :], misc[0:S, :], ACT.Tanh, scale=0.5, bias=b_g[:, :])\
                        .then_inc(s["g_done"], 1)
                elif at == 10:
                    act.wait_ge(s["uz_ps"], b + 1)
                    nc.scalar.activation(uz[:, :], misc[0:2 * S, :], ACT.Identity, bias=b_uz[:, :])\
                        .then_inc(s["uz_done"], 1)
                elif at == 11:
                    act.wait_ge(s["ut_ps"], b + 1)
                    nc.scalar.activation(u_tanh[:, :], misc[0:S, :], ACT.Tanh, bias=b_x_sb[:, :])\
                        .then_inc(s["ut_done"], 1)
                elif at == 12:
                    act.wait_ge(s["dt_ps"], b + 1)
                    nc.scalar.activation(dt_tanh[:, :], misc[0:S, :], ACT.Tanh, scale=0.5, bias=b_dt_sb[:, :])\
                        .then_inc(s["dt_done"], 1)
                elif at == 17:
                    to_channels(0, b, 0)
                elif at == 18:
                    ffn_r(0, b)
                elif at == 19:
                    ffn_k(0, b)
                elif at == 26:
                    to_channels(1, b, 1)
                elif at == 27:
                    act.wait_ge(s["q_ps"], b + 1)
                    nc.scalar.activation(qk_full[:, 0], misc[:, :], ACT.Copy, scale=HD ** -0.5)\
                        .then_inc(s["q_done"], 1)
                elif at == 28:
                    act.wait_ge(s["k_ps"], b + 1)
                    nc.scalar.activation(qk_full[:, 1], misc[:, :], ACT.Copy).then_inc(s["k_done"], 1)
                elif at == 29:
                    act.wait_ge(s["v_ps"], b + 1)
                    nc.scalar.activation(v_aug[:, q, :, :, 0:HD], misc[:, :].rearrange("p (t h d) -> p t h d", t=NT, h=H), ACT.Copy)\
                        .then_inc(s["v_done"], 1)

            def end(b, at):
                if at == 30:
                    act.wait_ge(s["oc_ps"], b + 1)
                    nc.scalar.activation(o_ch[:, :], misc[:, :], ACT.Copy).then_inc(s["oc_done"], 1)
                elif at == 34:
                    to_channels(2, b, 2)
                elif at == 35:
                    ffn_r(1, b)
                elif at == 36:
                    ffn_k(1, b)

            def body(i, p):
                for st in range(NG):
                    for k in range(NU):
                        at = NU * st + k
                        eb, _, g, G = group(i, st, 2)
                        if real(eb):
                            exps(G, k, g % 2)
                        mb, _, g, G = group(i, st, 1)
                        if k == 2 and real(mb):
                            act.wait_ge(s["max_ps"], G + 1)
                            if not isinstance(G, int) or G > 1:
                                act.wait_ge(s["max_loaded"], floor0(16 * HG * (G - 1)))
                            nc.scalar.activation(max_rows[:, g % 2], turn_b[0:HG * PARTS * NT, 0:P],
                                                 ACT.Copy).then_inc(s["max_copied"], 1)
                        pb, _, g, G = group(i, st, 3)
                        if k == 6 and real(pb):
                            act.wait_ge(s["turn_ready"], G)
                            act.wait_ge(s["pv_done"], G + 1)
                            nc.scalar.activation(o_heads[:, :], pv_bank[:, :], ACT.Copy)\
                                .then_inc(s["o_copied"], 1)
                        if real(i + 1):
                            front(i + 1, 1 - p, at)
                        if real(i - 1):
                            end(i - 1, at)

            iterations(act, body)

        @block.tensor
        def _(pe):
            def turn4(src, dst, done):
                for t in range(NT):
                    mm = pe.transpose(dst[:, P * t:P * (t + 1)], src[:, t], ident[:, :])
                mm.then_inc(s[done], 1)

            pe.wait_ge(s["c_silu_done"], 1)
            for n in range(2):
                pe.matmul(row_bank[n][0:NB, :], c_silu[:, n], wmod_sb[:, n, 0:4 * D], start=True, stop=True)
                mm = pe.matmul(col_bank[n][0:NB, 0:2 * D], c_silu[:, n], wmod_sb[:, n, 4 * D:6 * D],
                               start=True, stop=True)
            mm.then_inc(s["modrow_ps"], 1)
            for j, (n, k) in enumerate(((0, 4), (1, 1), (1, 4), (0, 3), (1, 0), (1, 3))):
                mm = pe.matmul(misc[:, NB * j:NB * (j + 1)], wmod_sb[:, n, D * k:D * (k + 1)], c_silu[:, n],
                               start=True, stop=True)
            mm.then_inc(s["modcol_ps"], 1)
            pe.wait_ge(s["pool_const"], 7)
            pe.wait_ge(s["vec_const"], 1)
            pe.wait_ge(s["mod_ready"], 1)

            def row_unit(i, p, g, k):
                n = NU * (NG * i + g) + k
                pe.wait_ge(s["row_read"], floor0(n - 1))
                dst = row_bank[k % 2]

                def scores(c0, t, half, tile, start):
                    rows = slice(HALF * half, HALF * half + KA)
                    pe.matmul(dst[:, c0:c0 + P * (tile + 1)], q_stack[rows, p, t, P * tile:P * (tile + 1)],
                              k_stack[rows, p, t, 0:P * (tile + 1)], start=start, stop=False,
                              skip_group_check=True)

                def mask(c0, m, stop):
                    return pe.matmul(dst[:, c0:c0 + P * m], identb[:, :],
                                     mask_q[:, 0:m, :].rearrange("p m c -> p (m c)"),
                                     start=False, stop=stop, skip_group_check=True)

                if k < 4:
                    scores(0, 2 * g + k // 2, k % 2, 3, True)
                    mm = mask(3 * P, 1, True)
                elif k < 8:
                    scores(0, 2 * g + (k - 4) // 2, k % 2, 2, True)
                    scores(3 * P, 2 * g + (k - 4) // 2, k % 2, 0, False)
                    mm = mask(2 * P, 2, True)
                else:
                    scores(0, 2 * g, k - 8, 1, True)
                    scores(2 * P, 2 * g + 1, k - 8, 1, False)
                    mask(P, 1, False)
                    mm = mask(3 * P, 1, True)
                mm.then_inc(s["row_ready"], 1)

            def col_unit(G, p, g, k):
                if k == 0:
                    pe.wait_ge(s["max_loaded"], 16 * HG * (G + 1))
                pe.wait_ge(s["exp_done"], floor0(NU * G + k - EXP_BACK[k] + 1))
                dst = col_bank[EXP_BANK[k]]

                def scores(c0, t, half, tile, start):
                    rows = slice(HALF * half, HALF * half + KB)
                    pe.matmul(dst[:, c0:c0 + L - P * tile], k_stack[rows, p, t, P * tile:P * (tile + 1)],
                              q_stack[rows, p, t, P * tile:L], start=start, stop=False,
                              skip_group_check=True)

                def mask(c0, m, stop):
                    return pe.matmul(dst[:, c0:c0 + P * m], identb[:, :],
                                     mask_k[:, 0:m, :].rearrange("p m c -> p (m c)"),
                                     start=False, stop=stop, skip_group_check=True)

                if k < 4:
                    scores(0, 2 * g + k // 2, k % 2, 0, True)
                    mm = mask(0, 1, True)
                elif k < 8:
                    scores(0, 2 * g + (k - 4) // 2, k % 2, 3, True)
                    scores(P, 2 * g + (k - 4) // 2, k % 2, 1, False)
                    mm = mask(0, 2, True)
                else:
                    scores(0, 2 * g, k - 8, 2, True)
                    scores(2 * P, 2 * g + 1, k - 8, 2, False)
                    mask(0, 1, False)
                    mm = mask(2 * P, 1, True)
                mm.then_inc(s["col_ready"], 1)

            def weigh(G, gp, p, g, tile):
                if tile == 0:
                    pe.wait_ge(s["exp_done"], NU * (G + 1))
                    pe.wait_ge(s["o_copied"], G)
                for k in range(HG):
                    if tile == 0:
                        src = probs[:, gp, k, :]
                    elif tile == 1:
                        src = probs[:, gp, 4 + k, P:]
                    elif tile == 3:
                        src = probs[:, gp, 4 + k, 0:P]
                    else:
                        src = probs[:, gp, 8 + k % 2, 2 * P * (k // 2):2 * P * (k // 2 + 1)]
                    mm = pe.matmul(pv_bank[32 * k:32 * (k + 1), P * tile:L], v_aug[:, p, tile, HG * g + k, :],
                                   src, start=(tile == 0), stop=(tile == NT - 1), skip_group_check=True)
                if tile == NT - 1:
                    mm.then_inc(s["pv_done"], 1)

            def ffn_r(n, b):
                pe.wait_ge(s[f"hc{2 * n}_done"], b + 1)
                hc = h_ch[2 * n]
                for t in range(NT):
                    pe.matmul(misc[:, P * t:P * (t + 1)], hc[:, 1 + P * t:1 + P * (t + 1)], ffn_now[:, n, 0],
                              start=True, stop=False)
                    mm = pe.matmul(misc[:, P * t:P * (t + 1)], hc[:, P * t:P * (t + 1)], ffn_prev[:, n, 0],
                                   start=False, stop=True)
                mm.then_inc(s[f"r{n}_ps"], 1)

            def ffn_k(n, b):
                pe.wait_ge(s[f"r{n}_done"], b + 1)
                hc = h_ch[2 * n]
                pe.matmul(misc[:, :], ffn_now[:, n, 1], hc[:, 1:1 + L], start=True, stop=False)
                pe.matmul(misc[:, :], ffn_prev[:, n, 1], hc[:, 0:L], start=False, stop=True)\
                    .then_inc(s[f"k{n}_ps"], 1)

            def by_tile(lhs, rhs, done):
                for t in range(NT):
                    mm = pe.matmul(misc[:, P * t:P * (t + 1)], lhs[:, P * t:P * (t + 1)], rhs,
                                   start=True, stop=True)
                mm.then_inc(s[done], 1)

            def front(b, q, at):
                if at == 8:
                    pe.wait_ge(s["hn_done"], b + 1)
                    turn4(h_norm, misc, "hn_ps")
                elif at == 9:
                    pe.wait_ge(s["hn_copied"], b + 1)
                    pe.matmul(misc[0:S, :], w_in_sb[:, 2 * S:3 * S], hn_ch[:, :],
                              start=True, stop=True).then_inc(s["g_ps"], 1)
                elif at == 10:
                    pe.wait_ge(s["g_done"], b + 1)
                    pe.matmul(misc[0:2 * S, :], w_in_sb[:, 0:2 * S], hn_ch[:, :],
                              start=True, stop=True).then_inc(s["uz_ps"], 1)
                elif at == 11:
                    pe.wait_ge(s["uz_done"], b + 1)
                    stand_alone(pe, b + 1)
                    pe.matmul(misc[0:S, :], w_xdt[0:S, :], uz[0:S, :],
                              start=True, stop=True).then_inc(s["ut_ps"], 1)
                elif at == 12:
                    pe.wait_ge(s["ut_done"], b + 1)
                    stand_alone(pe, b + 1)
                    pe.matmul(misc[0:S, :], w_xdt[S:2 * S, :], uz[S:2 * S, :],
                              start=True, stop=True).then_inc(s["dt_ps"], 1)
                elif at == 14:
                    pe.wait_ge(s["dt_done"], b + 1)
                    pe.wait_ge(s["y_done"], b + 1)
                    pe.wait_ge(s["wog_done"], b + 1)
                    by_tile(y, w_out_g[:, :], "out_ps")
                elif at == 17:
                    pe.wait_ge(s["x1_done"], b + 1)
                    pe.wait_ge(s["ln1_xhat"], NT * (b + 1))
                    turn4(x_hat[1], misc, "hc0_ps")
                elif at == 18:
                    ffn_r(0, b)
                elif at == 19:
                    ffn_k(0, b)
                elif at == 22:
                    pe.wait_ge(s["ksq0_done"], b + 1)
                    pe.wait_ge(s["wg0_done"], b + 1)
                    by_tile(k_sq[0], wv_g[0][:, 0], "kv0_ps")
                elif at == 26:
                    pe.wait_ge(s["kv0_done"], b + 1)
                    pe.wait_ge(s["ln2_xhat"], NT * (b + 1))
                    turn4(x_hat[2], misc, "hc1_ps")
                elif at == 27:
                    pe.wait_ge(s["hc1_done"], b + 1)
                    pe.matmul(misc[:, :], wq_sb[:, :], h_ch[1][:, 1:],
                              start=True, stop=True).then_inc(s["q_ps"], 1)
                elif at == 28:
                    pe.wait_ge(s["q_done"], b + 1)
                    pe.matmul(misc[:, :], wk_sb[:, :], h_ch[1][:, 1:],
                              start=True, stop=True).then_inc(s["k_ps"], 1)
                elif at == 29:
                    pe.wait_ge(s["k_done"], b + 1)
                    by_tile(h_ch[1][:, 1:], wv_sb[:, :], "v_ps")

            def end(b, p, at):
                if at == 30:
                    pe.wait_ge(s["o_norm"], NG * (b + 1))
                    if real(b + 2):
                        pe.wait_ge(s["v_done"], b + 3)
                    turn4(o_tok, misc, "oc_ps")
                elif at == 31:
                    pe.wait_ge(s["oc_done"], b + 1)
                    pe.wait_ge(s["wg1_done"], 2 * (b + 1))
                    by_tile(o_ch, wo_g[:, p], "wo_ps")
                elif at == 34:
                    pe.wait_ge(s["x3_done"], b + 1)
                    pe.wait_ge(s["ln3_xhat"], NT * (b + 1))
                    turn4(x_hat[3], misc, "hc2_ps")
                elif at == 35:
                    ffn_r(1, b)
                elif at == 36:
                    ffn_k(1, b)
                elif at == 38:
                    pe.wait_ge(s["ksq1_done"], b + 1)
                    by_tile(k_sq[1], wv_g[1][:, p], "kv1_ps")

            def body(i, p):
                for st in range(NG):
                    for k in range(NU):
                        at = NU * st + k
                        if real(i):
                            if at == 0:
                                pe.wait_ge(s["stacks_loaded"], 16 * LOADS * (i + 1))
                            row_unit(i, p, st, k)
                        b, dp, g, G = group(i, st, 2)
                        if real(b):
                            col_unit(G, (p + dp) % 2, g, k)
                        b, dp, g, G = group(i, st, 1)
                        if k == 2 and real(b):
                            pe.wait_ge(s["max_split"], G + 1)
                            pe.wait_ge(s["o_norm"], floor0(G - 2))
                            stand_alone(pe, G - 2)
                            pe.transpose(turn_b[0:HG * PARTS * NT, 0:P],
                                         max_part[:, :, :, :].rearrange("p h j t -> p (h j t)"),
                                         identb[:, :]).then_inc(s["max_ps"], 1)
                        b, dp, g, G = group(i, st, 3)
                        if real(b):
                            if 1 <= k <= NT:
                                weigh(G, g % 2, (p + dp) % 2, g, k - 1)
                            if k == 7:
                                pe.wait_ge(s["o_copied"], G + 1)
                                if real(group(i, st, 1)[0]):
                                    pe.wait_ge(s["max_copied"], G + 3)
                                pe.wait_ge(s["o_norm"], G)
                                turn4(tiles(o_heads[:, :]), turn, "turn_ready")
                        if real(i + 1):
                            front(i + 1, 1 - p, at)
                        if real(i - 1):
                            end(i - 1, 1 - p, at)

            iterations(pe, body)

        @block.vector
        def _(dve):
            nc.vector.memset(y[S:S + 1, :], 1.0).then_inc(s["y_ones"], 1)
            for n in range(3):
                nc.vector.memset(h_ch[n][:, 0:1], 0.0).then_inc(s["y_ones"], 1)
            for n in range(2):
                nc.vector.memset(v_aug[:, n, :, :, HD + 1:], 0.0).then_inc(s["y_ones"], 1)
                nc.vector.memset(v_aug[:, n, :, :, HD:HD + 1], 1.0).then_inc(s["y_ones"], 1)
            dve.wait_ge(s["c_tanh_done"], 1)
            nc.vector.scalar_tensor_tensor(c_silu[:, :, :], c_tanh[:, :, :], 1.0, c_sb[:, :, :], ALU.add,
                                           ALU.mult).then_inc(s["gate_step"], 1)
            dve.wait_ge(s["gate_step"], 1)
            nc.vector.tensor_scalar(c_silu[:, :, :], c_silu[:, :, :], 0.5, None, ALU.mult)\
                .then_inc(s["c_silu_done"], 1)
            dve.wait_ge(s["modrow_ps"], 1)
            nc.vector.tensor_copy(mod_row[:, 0], row_bank[0][0:NB, 0:D]).then_inc(s["gate_step"], 1)
            nc.vector.tensor_scalar(mod_row[:, 1], row_bank[0][0:NB, D:2 * D], 1.0, None, ALU.add)\
                .then_inc(s["gate_step"], 1)
            for n in range(2):
                nc.vector.tensor_copy(gate_raw[:, 2 * n], row_bank[n][0:NB, 2 * D:3 * D])\
                    .then_inc(s["gate_step"], 1)
                nc.vector.tensor_copy(gate_raw[:, 2 * n + 1], col_bank[n][0:NB, D:2 * D])\
                    .then_inc(s["gate_step"], 1)
            dve.wait_ge(s["gate_step"], 7)
            nc.vector.tensor_scalar(gate_sign[:, :, :], gate_raw[:, :, :], 0.0, 2.0, ALU.is_ge, ALU.mult)\
                .then_inc(s["gate_step"], 1)
            dve.wait_ge(s["gate_step"], 8)
            nc.vector.scalar_tensor_tensor(gate_abs, gate_sign, -1.0, gate_raw, ALU.add, ALU.mult)\
                .then_inc(s["gate_step"], 1)
            dve.wait_ge(s["gate_step"], 9)
            nc.vector.tensor_scalar(gate_size, gate_abs, 0.25, None, ALU.max).then_inc(s["gate_step"], 1)
            dve.wait_ge(s["gate_step"], 10)
            nc.vector.scalar_tensor_tensor(mod_row[:, 2:6], gate_sign[:, :, :], -1.0, gate_size[:, :, :],
                                           ALU.add, ALU.mult).then_inc(s["modrow_done"], 2)
            dve.wait_ge(s["modcol_ps"], 1)
            nc.vector.tensor_scalar(mod_col[:, 0:3], misc[:, 0:3 * NB].rearrange("p (k b) -> p k b", k=3),
                                    1.0, None, ALU.add).then_inc(s["gate_step"], 1)
            nc.vector.tensor_copy(mod_col[:, 3:6], misc[:, 3 * NB:6 * NB].rearrange("p (k b) -> p k b", k=3))\
                .then_inc(s["mod_ready"], 1)
            nc.vector.tensor_scalar(w_in_sb[:, :], w_in_sb[:, :], w_norm_sb[:, :], None, ALU.mult)\
                .then_inc(s["ffn_w_done"], 1)
            nc.vector.tensor_scalar(b_g[:, :], b_g[:, :], 0.5, None, ALU.mult).then_inc(s["ffn_w_done"], 1)
            nc.vector.tensor_scalar(b_dt_sb[:, :], b_dt_sb[:, :], 0.5, None, ALU.mult).then_inc(s["ffn_w_done"], 1)
            nc.vector.tensor_scalar(w_out_sb[0:S, :], w_out_sb[0:S, :], 0.25, None, ALU.mult)\
                .then_inc(s["ffn_w_done"], 1)
            for n in range(2):
                for j in range(2):
                    nc.vector.tensor_scalar(ffn_now[:, n, j], ffn_w[:, n, j], ffn_mu[:, n, j:j + 1], None,
                                            ALU.mult).then_inc(s["ffn_w_done"], 1)
            dve.wait_ge(s["ffn_w_done"], 8)
            for n in range(2):
                for j in range(2):
                    nc.vector.tensor_tensor(ffn_prev[:, n, j], ffn_w[:, n, j], ffn_now[:, n, j],
                                            ALU.subtract).then_inc(s["ffn_w_done"], 1)
                nc.vector.tensor_scalar(ffn_w[:, n, 2], ffn_w[:, n, 2], 0.5, None, ALU.mult)\
                    .then_inc(s["ffn_w_done"], 1)
            dve.wait_ge(s["ffn_w_done"], 14)
            dve.wait_ge(s["y_ones"], 8)
            dve.wait_ge(s["gate_step"], 11)
            dve.sem_inc(s["vec_const"], 1)

            def ln_stats(n, b, src):
                for t in range(NT):
                    nc.vector.bn_stats(stats[n][:, t], src[:, t]).then_inc(s[f"ln{n}_stat"], 1)
                dve.wait_ge(s[f"ln{n}_stat"], NT * (b + 1))
                stand_alone(dve, NT * (b + 1))
                for t in range(NT):
                    nc.vector.bn_aggr(mean_var[n][:, t], stats[n][:, t]).then_inc(s[f"ln{n}_mv"], 1)

            def recurrence(b):
                dve.wait_ge(s["dt_done"], b + 1)
                dve.wait_ge(s["ut_done"], b + 1)
                dve.wait_ge(s["g_done"], b + 1)
                nc.vector.tensor_scalar(keep[:, :], dt_tanh[:, :], -0.5, 0.5, ALU.mult, ALU.add)\
                    .then_inc(s["scan_step"], 1)
                nc.vector.scalar_tensor_tensor(feed[:, :], dt_tanh[:, :], 1.0, u_tanh[:, :], ALU.add,
                                               ALU.mult).then_inc(s["scan_step"], 1)
                dve.wait_ge(s["scan_step"], 3 * b + 2)
                nc.vector.tensor_tensor_scan(state[:, :], keep[:, :], feed[:, :], 0.0, ALU.mult, ALU.add)\
                    .then_inc(s["scan_step"], 1)
                dve.wait_ge(s["scan_step"], 3 * b + 3)
                nc.vector.scalar_tensor_tensor(y[0:S, :], g_tanh[:, :], 1.0, state[:, :], ALU.add,
                                               ALU.mult).then_inc(s["y_done"], 1)

            def ffn_gate(n, b):
                dve.wait_ge(s[f"kv{n}_ps"], b + 1)
                dve.wait_ge(s[f"r{n}_done"], b + 1)
                nc.vector.scalar_tensor_tensor(ffn_out[n][:, :, :], tiles(r_tanh[n][:, :]), 1.0,
                                               tiles(misc[:, :]), ALU.add, ALU.mult)\
                    .then_inc(s[f"kv{n}_done"], 1)

            def first_part(n, b):
                dve.wait_ge(s[("q_done", "k_done")[n]], b + 1)
                nc.vector.tensor_copy(qk_part[:, n, 0], qk_full[:, n]).then_inc(s["split_q1"], 1)

            def second_part(n, b):
                dve.wait_ge(s["split_r1"], 2 * b + n + 1)
                nc.vector.tensor_copy(qk_part[:, n, 1], qk_rest[:, n]).then_inc(s["split_q2"], 1)

            def row_max(G, gp, k):
                n = NU * G + k
                if k == 0:
                    dve.wait_ge(s["max_split"], floor0(G - 1))
                dve.wait_ge(s["row_ready"], n + 1)
                src, dst = row_bank[k % 2], neg_max[:, gp]
                if k < 4:
                    red = nc.vector.tensor_reduce(dst[:, k, 3:4], src[:, :], AX_X, ALU.max, negate=True)
                elif k < 8:
                    nc.vector.tensor_reduce(dst[:, k - 4, 2:3], src[:, 0:3 * P], AX_X, ALU.max, negate=True)
                    red = nc.vector.tensor_reduce(dst[:, k - 4, 0:1], src[:, 3 * P:], AX_X, ALU.max,
                                                  negate=True)
                else:
                    red = nc.vector.tensor_reduce(dst[:, k - 8::2, 1],
                                                  src[:, :].rearrange("p (h c) -> p h c", h=2), AX_X,
                                                  ALU.max, negate=True)
                red.then_inc(s["row_read"], 1)

            def normalize_heads(G, g):
                dve.wait_ge(s["turn_ready"], G + 1)
                heads = turn[:, :].rearrange("p (t h c) -> p t h c", t=NT, h=HG)
                nc.vector.tensor_tensor(denom[:, :, :], heads[:, :, :, HD],
                                        over(exp_bias[:, HG * g:HG * (g + 1)]), ALU.add)\
                    .then_inc(s["denom_step"], 1)
                dve.wait_ge(s["denom_step"], 2 * G + 1)
                nc.vector.reciprocal(denom_inv[:, :, :], denom[:, :, :]).then_inc(s["denom_step"], 1)
                dve.wait_ge(s["denom_step"], 2 * G + 2)
                dst = o_tok[:, :, D // NG * g:D // NG * (g + 1)].rearrange("p t (h d) -> p t h d", h=HG)
                nc.vector.tensor_tensor(dst, heads[:, :, :, 0:HD],
                                        denom_inv[:, :, :].unsqueeze(3).broadcast_to([P, NT, HG, HD]),
                                        ALU.mult).then_inc(s["o_norm"], 1)

            def front(b, q, at):
                if at == 2:
                    dve.wait_ge(s["x_loaded"], 16 * (b + 1))
                    ln_stats(0, b, x_in[:, q])
                elif at == 5:
                    dve.wait_ge(s["h_sq_done"], b + 1)
                    nc.vector.tensor_reduce(h_sum[:, :], h_sq[:, :, :], AX_X, ALU.add)\
                        .then_inc(s["h_sum_done"], 1)
                elif at == 13:
                    recurrence(b)
                elif at == 14:
                    dve.wait_ge(s["out_ps"], b + 1)
                    dve.wait_ge(s["xh_done"], b + 1)
                    nc.vector.tensor_tensor(x1[:, :, :], x_plus_h[:, :, :], tiles(misc[:, :]), ALU.add)\
                        .then_inc(s["x1_done"], 1)
                    dve.wait_ge(s["x1_done"], b + 1)
                    ln_stats(1, b, x1)
                elif at == 22:
                    ffn_gate(0, b)
                elif at == 24:
                    dve.wait_ge(s["x2_done"], b + 1)
                    ln_stats(2, b, x2)
                elif at == 27:
                    first_part(0, b)
                elif at == 28:
                    first_part(1, b)
                elif at == 30:
                    second_part(0, b)
                elif at == 31:
                    second_part(1, b)

            def end(b, p, at):
                if at == 32:
                    dve.wait_ge(s["wo_ps"], b + 1)
                    dve.wait_ge(s["xbo_done"], b + 1)
                    nc.vector.tensor_tensor(x3[:, :, :], x_bo[:, p], tiles(misc[:, :]), ALU.add)\
                        .then_inc(s["x3_done"], 1)
                    dve.wait_ge(s["x3_done"], b + 1)
                    ln_stats(3, b, x3)
                elif at == 39:
                    ffn_gate(1, b)

            def body(i, p):
                for st in range(NG):
                    for k in range(NU):
                        at = NU * st + k
                        if real(i):
                            row_max(NG * i + st, st % 2, k)
                            if k == NU - 1:
                                dve.wait_ge(s["row_read"], NU * (NG * i + st + 1))
                                dve.sem_inc(s["max_ready"], 1)
                        b, _, g, G = group(i, st, 3)
                        if k == 8 and real(b):
                            normalize_heads(G, g)
                        if real(i + 1):
                            front(i + 1, 1 - p, at)
                        if real(i - 1):
                            end(i - 1, 1 - p, at)

            iterations(dve, body)


N_WEIGHTS = 4 + 10 + 4 + 2 + 2 * 5

_INS = ["L0_attn_x", "L0_attn_W_in", "L0_attn_w_norm", "L0_attn_b_in", "L0_attn_W_x", "L0_attn_b_x",
        "L0_attn_W_dt", "L0_attn_b_dt", "L0_attn_W_out", "L0_attn_b_out"]
_FFN = ["W_r", "W_k", "W_v", "mu_r", "mu_k"]
_TURNED = ("W_r", "W_k", "W_v", "Wq", "Wk", "Wv", "Wo", "_c")


def kernel(**inputs):
    import numpy as _np
    import concourse.bacc as _bacc
    from concourse import mybir as _mybir
    from concourse.bass_utils import run_bass_kernel_spmd as _run

    nc = _bacc.Bacc("TRN2", target_bir_lowering=False, num_devices=1)
    arrays = {}

    def give(name):
        a = _np.asarray(inputs[name])
        if name.endswith(_TURNED):
            a = a.T
        a = _np.ascontiguousarray(a)
        arrays[f"in_{name}"] = a
        return nc.dram_tensor(f"in_{name}", a.shape, _mybir.dt.from_np(a.dtype), kind="ExternalInput").ap()

    layer0 = [give(n) for n in _INS]
    f0 = [give(f"L0_ffn_{n}") for n in _FFN]
    c0, wmod0 = give("L0_c"), give("L0_wmod")
    attn = [give(f"L1_attn_{n}") for n in ("Wq", "Wk", "Wv", "Wo", "bo", "denom_bias")]
    f1 = [give(f"L1_ffn_{n}") for n in _FFN]
    c1, wmod1 = give("L1_c"), give("L1_wmod")
    out = nc.dram_tensor("out", (NB, L, D), F32, kind="ExternalOutput").ap()
    build(nc, *layer0, f0, c0, wmod0, *attn, f1, c1, wmod1, out)
    r = _run(nc, [arrays], core_ids=[0])
    return r.results[0]["out"]
```

```python
from contextlib import ExitStack

import concourse.bass as bass
from concourse import mybir

ALU = mybir.AluOpType
ACT = mybir.ActivationFunctionType
AX_X = mybir.AxisListType.X
F32 = mybir.dt.float32
BF16 = mybir.dt.bfloat16

NB = 8
L = 512
D = 128
P = 128
NT = L // P
S = 32
H = 16
HD = D // H
HG = 4
NG = H // HG
NU = 10
HALF = 64
PARTS = 3
NS = PARTS * (PARTS + 1) // 2
KA = NS * HD
KB = KA + PARTS
NEG = -1.0e30
LOWEST = -3.0e38
LN_EPS = 1e-5
RMS_EPS = 1e-8
LOADS = 2 * (PARTS + 1)
READS = (1, 2, 3, 4, 6, 8, 10, 12, 14, 16)
NR = READS[-1]

WEIGH = ((0, 0, 256), (0, 256, 512), (1, 128, 320), (1, 320, 512), (2, 256, 512), (3, 384, 512))

PERIOD = NG * NU
DEPTH = 4
T_LOAD = 0
T_LN0 = 4
T_H = 6
T_RMS = 9
T_HN = 12
T_XH = 13
T_UZG = 14
T_UDT = 16
T_SCAN = 17
T_X1 = 19
T_HAT1 = 22
T_HC0 = 23
T_DIFF0 = 24
T_MIX0 = 26
T_R0 = 27
T_K0 = 29
T_KV0 = 31
T_LN2 = 33
T_HAT2 = 35
T_HC1 = 36
T_Q = 38
T_K = 40
T_V = 46
T_PARTS2 = 42
T_PARTS3 = 44
T_STACK = 46
T_ROW = 60
T_GATE1 = 60
T_GATE2 = 66
T_MAX = T_ROW + NU
T_COL = T_ROW + 2 * NU
T_PV = T_COL + NU + 1
T_TURN = T_PV + len(WEIGH)
T_OC = T_TURN + NU * (NG - 1) + 4
T_X3 = T_OC + 2
T_HAT3 = T_X3 + 3
T_HC2 = T_HAT3 + 1
T_DIFF1 = T_HC2 + 1
T_MIX1 = T_DIFF1 + 2
T_R1 = T_MIX1 + 1
T_K1 = T_R1 + 2
T_KV1 = T_K1 + 2
T_OUT = T_KV1 + 2
assert T_OUT < PERIOD * DEPTH


def build(nc, x, w_in, w_norm, b_in, w_x, b_x, w_dt, b_dt, w_out, b_out, f0, c0T, wmod0,
          wqT, wkT, wvT, woT, bo, denom_bias, f1, c1T, wmod1, out):
    ctx = ExitStack()
    with ctx:
        def sb(name, shape, dt=F32):
            return ctx.enter_context(nc.sbuf_tensor(name, shape, dt))

        def bank(name):
            return ctx.enter_context(nc.psum_tensor(name, [P, 512], F32))

        mod_dram = nc.dram_tensor("mod_rows", (NB, 6 * D), F32).ap()
        q_dram = nc.dram_tensor("q_parts", (2, PARTS, HD, H, L), BF16).ap()
        k_dram = nc.dram_tensor("k_parts", (2, NS, HD, H, L), BF16).ap()

        ident = sb("ident", [P, P])
        identb = sb("identb", [P, P], BF16)
        mask_row = sb("mask_row", [P, L], BF16)
        mask_col = sb("mask_col", [P, 2, P], BF16)
        neg_half = sb("neg_half", [P, NT])
        w_in_sb = sb("w_in_sb", [P, 3 * S])
        w_norm_sb = sb("w_norm_sb", [P, 1])
        b_uzg = sb("b_uzg", [3 * S, 1])
        w_xdt = sb("w_xdt", [2 * S, 2 * S])
        b_xdt = sb("b_xdt", [2 * S, 1])
        w_out_sb = sb("w_out_sb", [S + 1, D])
        c_sb = sb("c_sb", [P, 2, NB])
        c_tanh = sb("c_tanh", [P, 2, NB])
        c_silu = sb("c_silu", [P, 2, NB])
        wmod_sb = sb("wmod_sb", [P, 2, 6 * D])
        mod_col = sb("mod_col", [P, 6, NB])
        mod_row = sb("mod_row", [NB, 6, D])
        wq_sb = sb("wq_sb", [P, D])
        wk_sb = sb("wk_sb", [P, D])
        wv_sb = sb("wv_sb", [P, D])
        wo_sb = sb("wo_sb", [P, D])
        bo_sb = sb("bo_sb", [P, D])
        exp_bias = sb("exp_bias", [P, H])
        ffn_w = sb("ffn_w", [P, 2, 3, D])
        ffn_mu = sb("ffn_mu", [P, 2, 2])

        mod = sb("mod", [P, 2, 6, D])
        x_in = sb("x_in", [P, 2, NT, D])
        stats = [sb(f"stats{n}", [P, NT, 6]) for n in range(4)]
        mean_var = [sb(f"mean_var{n}", [P, NT, 2]) for n in range(4)]
        var_eps = [sb(f"var_eps{n}", [P, NT]) for n in range(4)]
        rstd = [sb(f"rstd{n}", [P, NT]) for n in range(4)]
        x_hat = [sb(f"x_hat{n}", [P, NT, D]) for n in range(4)]
        h_tok = sb("h_tok", [P, NT, D])
        h_sq = sb("h_sq", [P, NT, D])
        h_sum = sb("h_sum", [P, NT])
        h_mean = sb("h_mean", [P, NT])
        h_rms = sb("h_rms", [P, NT])
        h_norm = h_sq
        x_plus_h = x_hat[0]
        hn_ch = sb("hn_ch", [P, L])
        w_out_g = sb("w_out_g", [S + 1, D])
        g_tanh = sb("g_tanh", [S, L])
        uz = sb("uz", [2 * S, L])
        u_tanh = sb("u_tanh", [S, L])
        dt_tanh = sb("dt_tanh", [S, L])
        keep = sb("keep", [S, L])
        feed = sb("feed", [S, L])
        state = sb("state", [S, L])
        y = sb("y", [S + 1, L])
        gate_raw, gate_sign, gate_abs, gate_size = (t[0:NB, :].rearrange("b (k c) -> b k c", k=4)
                                                    for t in (keep, feed, state, u_tanh))
        x1 = sb("x1", [P, NT, D])
        x2 = sb("x2", [P, NT, D])
        x_bo = sb("x_bo", [P, 2, NT, D])
        g_bo = sb("g_bo", [P, D])
        x3 = sb("x3", [P, NT, D])
        x4 = sb("x4", [P, NT, D])
        wo_g = sb("wo_g", [P, 2, D])
        wv_g0 = sb("wv_g0", [P, D])
        wv_g1 = sb("wv_g1", [P, 2, D])
        h_ch = [sb(f"h_ch{n}", [P, 1 + L]) for n in range(3)]
        h_diff = [x_hat[1][:, :, :].rearrange("p t c -> p (t c)"), x_hat[3][:, :, :].rearrange("p t c -> p (t c)")]
        mix_k = h_diff
        ffn_out = [sb(f"ffn_out{n}", [P, NT, D]) for n in range(2)]
        mix_r = [t[:, :, :].rearrange("p t c -> p (t c)") for t in ffn_out]
        r_tanh = [sb(f"r_tanh{n}", [P, L]) for n in range(2)]
        k_sq = [sb(f"k_sq{n}", [P, L]) for n in range(2)]
        qk_full = sb("qk_full", [P, 2, L])
        qk_rest = sb("qk_rest", [P, 2, L])
        qk_part = sb("qk_part", [P, 2, PARTS, L], BF16)
        q_stack = sb("q_stack", [P, 2, H // 2, L], BF16)
        k_stack = sb("k_stack", [P, 2, H // 2, L], BF16)
        v_aug = sb("v_aug", [P, 2, NT, H, 32])
        row_max = sb("row_max", [P, 2, HG, NT])
        max_rest = sb("max_rest", [P, HG, NT])
        max_part = sb("max_part", [P, HG, PARTS, NT], BF16)
        max_rows = sb("max_rows", [HG * PARTS * NT, 2, P], BF16)
        probs = sb("probs", [P, 2, NU, 512])
        o_heads = sb("o_heads", [P, L])
        denom = sb("denom", [P, NT, HG])
        denom_inv = sb("denom_inv", [P, NT, HG])
        o_tok = sb("o_tok", [P, NT, D])
        o_ch = sb("o_ch", [P, L])

        row_bank = [bank(f"row_bank{n}") for n in range(2)]
        col_bank = [bank(f"col_bank{n}") for n in range(2)]
        pv_bank = bank("pv_bank")
        front = bank("front")
        end = bank("end")
        turn = bank("turn")
        turn_b = turn[:, :].bitcast(BF16)

        names = """w_loaded w_zero pool_zero pool_const vec_const vec_fill c_tanh_done c_silu_done
        modrow_ps modcol_ps mod_ready gate_step modrow_done mod_stored w_scaled bias_exp
        mod_loaded x_loaded
        ln0_stat ln0_mv ln0_rs ln0_hat ln1_stat ln1_mv ln1_rs ln1_hat
        ln2_stat ln2_mv ln2_rs ln2_hat ln3_stat ln3_mv ln3_rs ln3_hat
        h_scaled h_done h_sq_done h_sum_done rms_step hn_done gh_done xh_done wog_done wg0_done
        hn_ps hn_copied uzg_ps uz_done g_done udt_ps ut_done dt_done
        scan_step y_done out_ps x1_done
        hc0_ps hc0_done diff0_done mix0_done r0_ps r0_done k0_ps k0_done ksq0_done kv0_ps kv0_done x2_done
        hc1_ps hc1_done q_ps q_full k_ps k_full v_ps v_done
        part1_done rest_done part2_done part3_done parts_stored stacks_loaded
        gbo_done xbo_done wog1_done wg1_done
        row_ready row_read max_step max_split max_ps max_copied max_loaded
        col_ready exp_done pv_done o_copied turn_ready denom_step o_norm
        oc_ps oc_done wo_ps x3_done
        hc2_ps hc2_done diff1_done mix1_done r1_ps r1_done k1_ps k1_done ksq1_done kv1_ps kv1_done
        x4_done out_stored waited""".split()
        s = {name: ctx.enter_context(nc.semaphore(name)) for name in names}

        def floor0(count):
            return max(count, 0) if isinstance(count, int) else count

        def stand_alone(eng, count):
            if not isinstance(count, int):
                eng.sem_inc(s["waited"], 1)

        def over(t):
            return t.unsqueeze(1).broadcast_to([t.shape[0], NT, t.shape[1]])

        def along(t):
            return t.unsqueeze(2).broadcast_to([P, NT, D])

        def tiles(t):
            return t.rearrange("p (t c) -> p t c", t=NT)

        def group_at(T, start):
            if 0 <= T - start < PERIOD:
                return (T - start) // NU, (T - start) % NU
            return None, None

        def iterations(eng, stage):
            def body(i, parity):
                for slot in range(PERIOD):
                    for n in range(DEPTH):
                        b = i + 1 - n
                        if not isinstance(b, int) or 0 <= b < NB:
                            stage(b, (parity + 1 - n) % 2, PERIOD * n + slot)

            body(-1, 1)
            body(0, 0)
            body(1, 1)
            with eng.Fori(2, NB - 3, 2) as i:
                body(i, 0)
                body(i + 1, 1)
            for i in range(NB - 2, NB + DEPTH - 2):
                body(i, i % 2)

        block = ctx.enter_context(nc.Block())

        @block.sync
        def _(sp):
            def load(dst, src, name):
                sp.dma_start(dst, src).then_inc(s[name], 16)

            def col(v, lo, hi):
                return v[lo:hi].rearrange("(p o) -> p o", o=1)

            def load_x(b, q):
                load(x_in[:, q], x[bass.ds(b, 1)].rearrange("o (t p) c -> p (o t) c", p=P), "x_loaded")

            sp.sem_inc(s["out_stored"], 16)
            load(c_sb[:, 0], c0T, "w_loaded")
            load(c_sb[:, 1], c1T, "w_loaded")
            load(wmod_sb[:, 0], wmod0, "w_loaded")
            load(wmod_sb[:, 1], wmod1, "w_loaded")
            load_x(0, 0)
            load(w_in_sb[:, :], w_in, "w_loaded")
            load(w_norm_sb[:, :], col(w_norm, 0, D), "w_loaded")
            load(b_uzg[:, :], col(b_in, 0, 3 * S), "w_loaded")
            sp.wait_ge(s["w_zero"], 1)
            load(w_xdt[0:S, 0:S], w_x, "w_loaded")
            load(w_xdt[S:2 * S, S:2 * S], w_dt, "w_loaded")
            load(b_xdt[0:S, :], col(b_x, 0, S), "w_loaded")
            load(b_xdt[S:2 * S, :], col(b_dt, 0, S), "w_loaded")
            load(w_out_sb[0:S, :], w_out, "w_loaded")
            load(w_out_sb[S:S + 1, :], b_out.rearrange("(o n) -> o n", o=1), "w_loaded")
            for dst, src in ((wq_sb, wqT), (wk_sb, wkT), (wv_sb, wvT), (wo_sb, woT)):
                load(dst[:, :], src, "w_loaded")
            load(bo_sb[:, :], bo.partition_broadcast(P), "w_loaded")
            load(exp_bias[:, :], denom_bias.rearrange("a h b c -> (a h b c)").partition_broadcast(P), "w_loaded")
            for n, f in enumerate((f0, f1)):
                for j in range(3):
                    load(ffn_w[:, n, j], f[j], "w_loaded")
                for j in range(2):
                    load(ffn_mu[:, n, j:j + 1], col(f[3 + j], 0, D), "w_loaded")
            sp.wait_ge(s["modrow_done"], 1)
            load(mod_dram.rearrange("b (k c) -> b k c", k=6), mod_row[:, :, :], "mod_stored")
            sp.wait_ge(s["mod_stored"], 16)
            sp.wait_ge(s["pool_const"], 7)

            def stage(b, q, T):
                if T == T_LOAD:
                    if not isinstance(b, int) or b > 0:
                        sp.wait_ge(s["xh_done"], floor0(b - 1))
                        stand_alone(sp, b)
                        sp.wait_ge(s["x_loaded"], 16 * b)
                        stand_alone(sp, b)
                        load_x(b, q)
                        sp.wait_ge(s["mod_loaded"], 16 * b)
                        stand_alone(sp, b)
                    sp.wait_ge(s["wog1_done"], floor0(b - 1))
                    stand_alone(sp, b)
                    sp.wait_ge(s["wg1_done"], floor0(b - 1))
                    stand_alone(sp, b)
                    row = mod_dram[bass.ds(b, 1), :].rearrange("o n -> (o n)").partition_broadcast(P)
                    load(mod[:, q].rearrange("p k c -> p (k c)"), row, "mod_loaded")
                if T == T_STACK:
                    sp.wait_ge(s["part1_done"], 2 * (b + 1))
                    stand_alone(sp, b)
                    sp.wait_ge(s["part2_done"], 2 * (b + 1))
                    stand_alone(sp, b)
                    sp.wait_ge(s["part3_done"], 2 * (b + 1))
                    stand_alone(sp, b)
                    load(q_dram[q].rearrange("j d h l -> (d h) j l"), qk_part[:, 0], "parts_stored")
                    slot = 0
                    for part in range(PARTS):
                        n = PARTS - part
                        load(k_dram[q, slot:slot + n].rearrange("j d h l -> (d h) j l"),
                             qk_part[:, 1, part].unsqueeze(1).broadcast_to([P, n, L]), "parts_stored")
                        slot += n
                    sp.wait_ge(s["parts_stored"], 16 * (1 + PARTS) * (b + 1))
                    stand_alone(sp, b)
                    sp.wait_ge(s["stacks_loaded"], 16 * LOADS * b)
                    stand_alone(sp, b)
                    sp.wait_ge(s["col_ready"], floor0(NU * NG * (b - 1)))
                    stand_alone(sp, b)
                    for half in range(2):
                        load(k_stack[HALF * half:HALF * half + KA, q],
                             k_dram[q].rearrange("j d (t s) l -> s (j d) t l", s=2)[half], "stacks_loaded")
                        row = HALF * half
                        for n in range(PARTS, 0, -1):
                            load(q_stack[row:row + HD * n, q],
                                 q_dram[q, 0:n].rearrange("j d (t s) l -> s (j d) t l", s=2)[half],
                                 "stacks_loaded")
                            row += HD * n
                g, k = group_at(T, T_MAX)
                if k == 3:
                    G = NG * b + g
                    sp.wait_ge(s["max_loaded"], 16 * HG * G)
                    stand_alone(sp, G)
                    sp.wait_ge(s["max_copied"], G + 1)
                    stand_alone(sp, G)
                    for head in range(HG):
                        t, half = 2 * g + head // 2, head % 2
                        n = PARTS * NT * head
                        load(q_stack[HALF * half + KA:HALF * half + KB, q, t, :],
                             max_rows[n:n + PARTS * NT, g % 2, :], "max_loaded")
                if T == T_OUT:
                    sp.wait_ge(s["x4_done"], b + 1)
                    stand_alone(sp, b)
                    dst = out[bass.ds(b, 1)].rearrange("o (t p) c -> p (o t) c", p=P)
                    load(dst, x4[:, :, :], "out_stored")

            iterations(sp, stage)
            sp.wait_ge(s["out_stored"], 16 * (NB + 1))

        @block.gpsimd
        def _(pool):
            nc.gpsimd.memset(w_xdt[:, :], 0.0).then_inc(s["w_zero"], 1)
            nc.gpsimd.memset(ident[:, :], 0.0).then_inc(s["pool_zero"], 1)
            nc.gpsimd.memset(identb[:, :], 0.0).then_inc(s["pool_zero"], 1)
            nc.gpsimd.memset(mask_row[:, :], 0.0).then_inc(s["pool_zero"], 1)
            nc.gpsimd.memset(mask_col[:, :, :], 0.0).then_inc(s["pool_zero"], 1)
            pool.wait_ge(s["pool_zero"], 4)
            for m in (ident, identb):
                nc.gpsimd.affine_select(m[:, :], m[:, :], [[-1, P]], ALU.not_equal, 1.0, base=0,
                                        channel_multiplier=1).then_inc(s["pool_const"], 1)
            nc.gpsimd.affine_select(mask_row[:, L - P:], mask_row[:, L - P:], [[-1, P]], ALU.is_ge, NEG,
                                    base=0, channel_multiplier=1).then_inc(s["pool_const"], 1)
            nc.gpsimd.affine_select(mask_col[:, :, :], mask_col[:, :, :], [[0, 2], [1, P]], ALU.is_ge, NEG,
                                    base=0, channel_multiplier=-1).then_inc(s["pool_const"], 1)
            nc.gpsimd.memset(neg_half[:, :], -0.5).then_inc(s["pool_const"], 1)
            nc.gpsimd.memset(k_stack[:, 0], -1.0).then_inc(s["pool_const"], 1)
            nc.gpsimd.memset(k_stack[:, 1], -1.0).then_inc(s["pool_const"], 1)
            pool.wait_ge(s["pool_const"], 7)

            def inv_std(n, b):
                pool.wait_ge(s[f"ln{n}_mv"], NT * (b + 1))
                stand_alone(pool, b)
                nc.gpsimd.tensor_scalar(var_eps[n][:, :], mean_var[n][:, :, 1], LN_EPS, None,
                                        ALU.add).then_inc(s[f"ln{n}_rs"], 1)
                pool.wait_ge(s[f"ln{n}_rs"], 2 * b + 1)
                stand_alone(pool, b)
                nc.gpsimd.tensor_tensor(rstd[n][:, :], var_eps[n][:, :], neg_half[:, :],
                                        ALU.pow).then_inc(s[f"ln{n}_rs"], 1)

            def diff(n, b):
                pool.wait_ge(s[f"hc{2 * n}_done"], b + 1)
                stand_alone(pool, b)
                nc.gpsimd.tensor_tensor(h_diff[n], h_ch[2 * n][:, 1:1 + L], h_ch[2 * n][:, 0:L],
                                        ALU.subtract).then_inc(s[f"diff{n}_done"], 1)

            def rest(n, b):
                pool.wait_ge(s["part1_done"], 2 * b + n + 1)
                stand_alone(pool, b)
                nc.gpsimd.tensor_tensor(qk_rest[:, n], qk_full[:, n], qk_part[:, n, 0],
                                        ALU.subtract).then_inc(s["rest_done"], 1)

            def last_part(n, b):
                pool.wait_ge(s["part2_done"], 2 * b + n + 1)
                stand_alone(pool, b)
                nc.gpsimd.tensor_tensor(qk_part[:, n, 2], qk_rest[:, n], qk_part[:, n, 1],
                                        ALU.subtract).then_inc(s["part3_done"], 1)

            def max_parts(G, gp):
                pool.wait_ge(s["row_read"], NR * (G + 1))
                stand_alone(pool, G)
                pool.wait_ge(s["max_ps"], G)
                stand_alone(pool, G)
                full = row_max[:, gp]
                nc.gpsimd.tensor_copy(max_part[:, :, 0, :], full).then_inc(s["max_step"], 1)
                pool.wait_ge(s["max_step"], 3 * G + 1)
                stand_alone(pool, G)
                nc.gpsimd.tensor_tensor(max_rest[:, :, :], full, max_part[:, :, 0, :],
                                        ALU.subtract).then_inc(s["max_step"], 1)
                pool.wait_ge(s["max_step"], 3 * G + 2)
                stand_alone(pool, G)
                nc.gpsimd.tensor_copy(max_part[:, :, 1, :], max_rest[:, :, :]).then_inc(s["max_step"], 1)
                pool.wait_ge(s["max_step"], 3 * G + 3)
                stand_alone(pool, G)
                nc.gpsimd.tensor_tensor(max_part[:, :, 2, :], max_rest[:, :, :], max_part[:, :, 1, :],
                                        ALU.subtract).then_inc(s["max_split"], 1)

            pool.wait_ge(s["vec_const"], 1)

            def stage(b, q, T):
                g, k = group_at(T, T_MAX)
                if k == 0:
                    max_parts(NG * b + g, g % 2)
                if T == T_LN0:
                    inv_std(0, b)
                elif T == T_H:
                    pool.wait_ge(s["ln0_hat"], NT * (b + 1))
                    stand_alone(pool, b)
                    pool.wait_ge(s["mod_loaded"], 16 * (b + 1))
                    stand_alone(pool, b)
                    nc.gpsimd.tensor_tensor(x_hat[0][:, :, :], x_hat[0][:, :, :], over(mod[:, q, 1]),
                                            ALU.mult).then_inc(s["h_scaled"], 1)
                    pool.wait_ge(s["h_scaled"], b + 1)
                    stand_alone(pool, b)
                    nc.gpsimd.tensor_tensor(h_tok[:, :, :], x_hat[0][:, :, :], over(mod[:, q, 0]),
                                            ALU.add).then_inc(s["h_done"], 1)
                elif T == T_RMS:
                    pool.wait_ge(s["h_sum_done"], b + 1)
                    stand_alone(pool, b)
                    nc.gpsimd.tensor_scalar(h_mean[:, :], h_sum[:, :], 1.0 / D, RMS_EPS, ALU.mult,
                                            ALU.add).then_inc(s["rms_step"], 1)
                    pool.wait_ge(s["rms_step"], 2 * b + 1)
                    stand_alone(pool, b)
                    nc.gpsimd.tensor_tensor(h_rms[:, :], h_mean[:, :], neg_half[:, :],
                                            ALU.pow).then_inc(s["rms_step"], 1)
                    pool.wait_ge(s["rms_step"], 2 * b + 2)
                    stand_alone(pool, b)
                    nc.gpsimd.tensor_tensor(h_norm[:, :, :], h_tok[:, :, :], along(h_rms[:, :]),
                                            ALU.mult).then_inc(s["hn_done"], 1)
                elif T == T_XH:
                    nc.gpsimd.tensor_tensor(x_hat[0][:, :, :], h_tok[:, :, :], over(mod[:, q, 2]),
                                            ALU.mult).then_inc(s["gh_done"], 1)
                    pool.wait_ge(s["gh_done"], b + 1)
                    stand_alone(pool, b)
                    nc.gpsimd.tensor_tensor(x_plus_h[:, :, :], x_hat[0][:, :, :], x_in[:, q],
                                            ALU.add).then_inc(s["xh_done"], 1)
                    nc.gpsimd.tensor_tensor(w_out_g[:, :], w_out_sb[:, :], mod[0:S + 1, q, 2],
                                            ALU.mult).then_inc(s["wog_done"], 1)
                    nc.gpsimd.tensor_tensor(wv_g0[:, :], ffn_w[:, 0, 2], mod[:, q, 3],
                                            ALU.mult).then_inc(s["wg0_done"], 1)
                elif T == T_X1:
                    inv_std(1, b)
                elif T == T_DIFF0:
                    diff(0, b)
                elif T == T_KV0:
                    pool.wait_ge(s["kv0_done"], b + 1)
                    stand_alone(pool, b)
                    nc.gpsimd.tensor_tensor(x2[:, :, :], x1[:, :, :], ffn_out[0][:, :, :],
                                            ALU.add).then_inc(s["x2_done"], 1)
                elif T == T_LN2:
                    inv_std(2, b)
                elif T == T_Q:
                    rest(0, b)
                elif T == T_K:
                    rest(1, b)
                elif T == T_PARTS3:
                    last_part(0, b)
                    last_part(1, b)
                elif T == T_GATE1:
                    pool.wait_ge(s["x2_done"], b + 1)
                    stand_alone(pool, b)
                    nc.gpsimd.tensor_tensor(g_bo[:, :], bo_sb[:, :], mod[:, q, 4],
                                            ALU.mult).then_inc(s["gbo_done"], 1)
                    pool.wait_ge(s["gbo_done"], b + 1)
                    stand_alone(pool, b)
                    nc.gpsimd.tensor_tensor(x_bo[:, q], x2[:, :, :], over(g_bo[:, :]),
                                            ALU.add).then_inc(s["xbo_done"], 1)
                    nc.gpsimd.tensor_tensor(wo_g[:, q], wo_sb[:, :], mod[:, q, 4],
                                            ALU.mult).then_inc(s["wog1_done"], 1)
                elif T == T_GATE2:
                    nc.gpsimd.tensor_tensor(wv_g1[:, q], ffn_w[:, 1, 2], mod[:, q, 5],
                                            ALU.mult).then_inc(s["wg1_done"], 1)
                elif T == T_X3:
                    inv_std(3, b)
                elif T == T_DIFF1:
                    diff(1, b)
                elif T == T_KV1:
                    pool.wait_ge(s["kv1_done"], b + 1)
                    stand_alone(pool, b)
                    pool.wait_ge(s["out_stored"], 16 * (b + 1))
                    stand_alone(pool, b)
                    nc.gpsimd.tensor_tensor(x4[:, :, :], x3[:, :, :], ffn_out[1][:, :, :],
                                            ALU.add).then_inc(s["x4_done"], 1)

            iterations(pool, stage)

        @block.scalar
        def _(act):
            act.wait_ge(s["w_loaded"], 16 * N_WEIGHTS)
            nc.scalar.activation(c_tanh[:, :, :], c_sb[:, :, :], ACT.Tanh, scale=0.5).then_inc(s["c_tanh_done"], 1)
            nc.scalar.activation(exp_bias[:, :], exp_bias[:, :], ACT.Exp).then_inc(s["bias_exp"], 1)
            act.wait_ge(s["vec_const"], 1)
            act.wait_ge(s["mod_ready"], 1)

            def to_channels(n, b, src):
                act.wait_ge(s[f"hc{n}_ps"], b + 1)
                nc.scalar.activation(h_ch[n][:, 1:1 + L], src[:, :], ACT.Identity,
                                     scale=mod_col[:, n, bass.ds(b, 1)],
                                     bias=mod_col[:, n + 3, bass.ds(b, 1)]).then_inc(s[f"hc{n}_done"], 1)

            def ffn_r(n, b, src):
                act.wait_ge(s[f"r{n}_ps"], b + 1)
                nc.scalar.activation(r_tanh[n][:, :], src[:, :], ACT.Tanh, scale=0.5)\
                    .then_inc(s[f"r{n}_done"], 1)

            def ffn_k(n, b, src):
                act.wait_ge(s[f"k{n}_ps"], b + 1)
                nc.scalar.activation(k_sq[n][:, :], src[:, :], ACT.Relu).then_inc(s[f"k{n}_done"], 1)
                act.wait_ge(s[f"k{n}_done"], b + 1)
                nc.scalar.activation(k_sq[n][:, :], k_sq[n][:, :], ACT.Square).then_inc(s[f"ksq{n}_done"], 1)

            def first_part(n, b):
                act.wait_ge(s[("q_full", "k_full")[n]], b + 1)
                nc.scalar.activation(qk_part[:, n, 0], qk_full[:, n], ACT.Copy).then_inc(s["part1_done"], 1)

            def second_part(n, b):
                act.wait_ge(s["rest_done"], 2 * b + n + 1)
                nc.scalar.activation(qk_part[:, n, 1], qk_rest[:, n], ACT.Copy).then_inc(s["part2_done"], 1)

            def stage(b, q, T):
                g, k = group_at(T, T_COL)
                if k is not None:
                    G = NG * b + g
                    if k == 0:
                        act.wait_ge(s["pv_done"], floor0(G - 1))
                    act.wait_ge(s["col_ready"], NU * G + k + 1)
                    nc.scalar.activation(probs[:, g % 2, k], col_bank[k % 2][:, :], ACT.Exp)\
                        .then_inc(s["exp_done"], 1)
                if T == T_RMS:
                    act.wait_ge(s["h_done"], b + 1)
                    nc.scalar.activation(h_sq[:, :, :], h_tok[:, :, :], ACT.Square).then_inc(s["h_sq_done"], 1)
                elif T == T_HN:
                    act.wait_ge(s["hn_ps"], b + 1)
                    nc.scalar.activation(hn_ch[:, :], front[:, :], ACT.Copy).then_inc(s["hn_copied"], 1)
                elif T == T_UZG:
                    act.wait_ge(s["uzg_ps"], b + 1)
                    nc.scalar.activation(uz[:, :], front[0:2 * S, :], ACT.Identity, bias=b_uzg[0:2 * S, :])\
                        .then_inc(s["uz_done"], 1)
                    nc.scalar.activation(g_tanh[:, :], front[2 * S:3 * S, :], ACT.Tanh, scale=0.5,
                                         bias=b_uzg[2 * S:3 * S, :]).then_inc(s["g_done"], 1)
                elif T == T_UDT:
                    act.wait_ge(s["udt_ps"], b + 1)
                    nc.scalar.activation(dt_tanh[:, :], front[S:2 * S, :], ACT.Tanh, scale=0.5,
                                         bias=b_xdt[S:2 * S, :]).then_inc(s["dt_done"], 1)
                    nc.scalar.activation(u_tanh[:, :], front[0:S, :], ACT.Tanh, bias=b_xdt[0:S, :])\
                        .then_inc(s["ut_done"], 1)
                elif T == T_HC0:
                    to_channels(0, b, front)
                elif T == T_R0:
                    ffn_r(0, b, front)
                elif T == T_K0:
                    ffn_k(0, b, front)
                elif T == T_HC1:
                    to_channels(1, b, front)
                elif T == T_Q:
                    act.wait_ge(s["q_ps"], b + 1)
                    nc.scalar.activation(qk_full[:, 0], front[:, :], ACT.Copy, scale=HD ** -0.5)\
                        .then_inc(s["q_full"], 1)
                    first_part(0, b)
                elif T == T_K:
                    act.wait_ge(s["k_ps"], b + 1)
                    nc.scalar.activation(qk_full[:, 1], front[:, :], ACT.Copy).then_inc(s["k_full"], 1)
                    first_part(1, b)
                elif T == T_V:
                    act.wait_ge(s["pv_done"], floor0(NG * (b - 1)))
                    act.wait_ge(s["v_ps"], b + 1)
                    nc.scalar.activation(v_aug[:, q, :, :, 0:HD],
                                         front[:, :].rearrange("p (t h d) -> p t h d", t=NT, h=H),
                                         ACT.Copy).then_inc(s["v_done"], 1)
                elif T == T_PARTS2:
                    second_part(0, b)
                    second_part(1, b)
                elif T == T_OC:
                    act.wait_ge(s["oc_ps"], b + 1)
                    nc.scalar.activation(o_ch[:, :], end[:, :], ACT.Copy).then_inc(s["oc_done"], 1)
                elif T == T_HC2:
                    to_channels(2, b, end)
                elif T == T_R1:
                    ffn_r(1, b, end)
                elif T == T_K1:
                    ffn_k(1, b, end)
                g, k = group_at(T, T_MAX)
                if k == 3:
                    G = NG * b + g
                    act.wait_ge(s["max_loaded"], floor0(16 * HG * (G - 1)))
                    act.wait_ge(s["max_ps"], G + 1)
                    nc.scalar.activation(max_rows[:, g % 2], turn_b[0:HG * PARTS * NT, 0:P],
                                         ACT.Copy).then_inc(s["max_copied"], 1)
                g, k = group_at(T, T_TURN)
                if k == 0:
                    G = NG * b + g
                    act.wait_ge(s["turn_ready"], G)
                    act.wait_ge(s["pv_done"], G + 1)
                    nc.scalar.activation(o_heads[:, :], pv_bank[:, :], ACT.Copy).then_inc(s["o_copied"], 1)

            iterations(act, stage)

        @block.tensor
        def _(pe):
            def turn4(src, dst, done):
                for t in range(NT):
                    mm = pe.transpose(dst[:, P * t:P * (t + 1)], src[:, t], ident[:, :])
                mm.then_inc(s[done], 1)

            def by_tile(dst, lhs, rhs, done):
                for t in range(NT):
                    mm = pe.matmul(dst[:, P * t:P * (t + 1)], lhs[:, P * t:P * (t + 1)], rhs,
                                   start=True, stop=True)
                mm.then_inc(s[done], 1)

            pe.wait_ge(s["c_silu_done"], 1)
            for n in range(2):
                pe.matmul(row_bank[n][0:NB, :], c_silu[:, n], wmod_sb[:, n, 0:4 * D], start=True, stop=True)
                mm = pe.matmul(col_bank[n][0:NB, 0:2 * D], c_silu[:, n], wmod_sb[:, n, 4 * D:6 * D],
                               start=True, stop=True)
            mm.then_inc(s["modrow_ps"], 1)
            for j, (n, k) in enumerate(((0, 4), (1, 1), (1, 4), (0, 3), (1, 0), (1, 3))):
                mm = pe.matmul(front[:, NB * j:NB * (j + 1)], wmod_sb[:, n, D * k:D * (k + 1)], c_silu[:, n],
                               start=True, stop=True)
            mm.then_inc(s["modcol_ps"], 1)
            pe.wait_ge(s["pool_const"], 7)
            pe.wait_ge(s["vec_const"], 1)
            pe.wait_ge(s["mod_ready"], 1)

            def row_unit(b, q, g, k):
                G = NG * b + g
                read = NR * G + READS[k - 2] if k >= 2 else NR * (G - 1) + READS[NU - 2 + k]
                pe.wait_ge(s["row_read"], floor0(read))
                dst = row_bank[k % 2]

                def scores(c0, t, half, tile, start, stop):
                    rows = slice(HALF * half, HALF * half + KA)
                    return pe.matmul(dst[:, c0:c0 + P * (tile + 1)],
                                     q_stack[rows, q, t, P * tile:P * (tile + 1)],
                                     k_stack[rows, q, t, 0:P * (tile + 1)], start=start, stop=stop,
                                     skip_group_check=True)

                if k < 4:
                    mm = scores(0, 2 * g + k // 2, k % 2, 3, True, True)
                elif k < 8:
                    scores(0, 2 * g + (k - 4) // 2, k % 2, 2, True, False)
                    mm = scores(3 * P, 2 * g + (k - 4) // 2, k % 2, 0, False, True)
                else:
                    scores(0, 2 * g, k - 8, 1, True, False)
                    mm = scores(2 * P, 2 * g + 1, k - 8, 1, False, True)
                mm.then_inc(s["row_ready"], 1)

            def col_unit(b, q, g, k):
                G = NG * b + g
                if k == 0:
                    pe.wait_ge(s["max_loaded"], 16 * HG * (G + 1))
                pe.wait_ge(s["exp_done"], floor0(NU * G + k - 1))
                dst = col_bank[k % 2]

                def scores(c0, t, half, tile, start):
                    rows = slice(HALF * half, HALF * half + KB)
                    pe.matmul(dst[:, c0:c0 + L - P * tile], k_stack[rows, q, t, P * tile:P * (tile + 1)],
                              q_stack[rows, q, t, P * tile:L], start=start, stop=False,
                              skip_group_check=True)

                def mask(c0, m, stop):
                    return pe.matmul(dst[:, c0:c0 + P * m], identb[:, :],
                                     mask_col[:, 0:m, :].rearrange("p m c -> p (m c)"),
                                     start=False, stop=stop, skip_group_check=True)

                if k < 4:
                    scores(0, 2 * g + k // 2, k % 2, 0, True)
                    mm = mask(0, 1, True)
                elif k < 8:
                    scores(0, 2 * g + (k - 4) // 2, k % 2, 3, True)
                    scores(P, 2 * g + (k - 4) // 2, k % 2, 1, False)
                    mm = mask(0, 2, True)
                else:
                    scores(0, 2 * g, k - 8, 2, True)
                    scores(2 * P, 2 * g + 1, k - 8, 2, False)
                    mask(0, 1, False)
                    mm = mask(2 * P, 1, True)
                mm.then_inc(s["col_ready"], 1)

            def weigh(b, q, g, k):
                G = NG * b + g
                tile, lo, hi = WEIGH[k]
                if k == 0:
                    pe.wait_ge(s["o_copied"], G)
                    pe.wait_ge(s["exp_done"], NU * (G + 1))
                for head in range(HG):
                    unit, at = ((head, 0), (4 + head, 0), (8 + head % 2, 2 * P * (head // 2) - 2 * P),
                                (4 + head, -3 * P))[tile]
                    mm = pe.matmul(pv_bank[32 * head:32 * (head + 1), lo:hi],
                                   v_aug[:, q, tile, HG * g + head, :],
                                   probs[:, g % 2, unit, at + lo:at + hi],
                                   start=(k == 0), stop=(k == len(WEIGH) - 1), skip_group_check=True)
                if k == len(WEIGH) - 1:
                    mm.then_inc(s["pv_done"], 1)

            def ffn_r(n, b, dst):
                pe.wait_ge(s[f"mix{n}_done"], 2 * (b + 1))
                by_tile(dst, mix_r[n], ffn_w[:, n, 0], f"r{n}_ps")

            def ffn_k(n, b, dst):
                pe.wait_ge(s[f"r{n}_done"], b + 1)
                pe.matmul(dst[:, :], ffn_w[:, n, 1], mix_k[n], start=True, stop=True).then_inc(s[f"k{n}_ps"], 1)

            def stage(b, q, T):
                g, k = group_at(T, T_ROW)
                if k is not None:
                    if T == T_ROW:
                        pe.wait_ge(s["stacks_loaded"], 16 * LOADS * (b + 1))
                    row_unit(b, q, g, k)
                g, k = group_at(T, T_COL)
                if k is not None:
                    col_unit(b, q, g, k)
                g, k = group_at(T, T_MAX)
                if k == 3:
                    G = NG * b + g
                    pe.wait_ge(s["o_norm"], floor0(G - 2))
                    pe.wait_ge(s["max_split"], G + 1)
                    stand_alone(pe, G)
                    pe.transpose(turn_b[0:HG * PARTS * NT, 0:P],
                                 max_part[:, :, :, :].rearrange("p h j t -> p (h j t)"),
                                 identb[:, :]).then_inc(s["max_ps"], 1)
                g, k = group_at(T, T_PV)
                if k is not None and k < len(WEIGH):
                    weigh(b, q, g, k)
                g, k = group_at(T, T_TURN)
                if k == 1:
                    G = NG * b + g
                    pe.wait_ge(s["max_copied"], min(G + 3, NG * NB) if isinstance(G, int) else G + 3)
                    pe.wait_ge(s["o_norm"], G)
                    pe.wait_ge(s["o_copied"], G + 1)
                    turn4(tiles(o_heads[:, :]), turn, "turn_ready")
                if T == T_HN:
                    pe.wait_ge(s["v_done"], b)
                    pe.wait_ge(s["hn_done"], b + 1)
                    turn4(h_norm, front, "hn_ps")
                elif T == T_UZG:
                    pe.wait_ge(s["hn_copied"], b + 1)
                    pe.matmul(front[0:3 * S, :], w_in_sb[:, :], hn_ch[:, :],
                              start=True, stop=True).then_inc(s["uzg_ps"], 1)
                elif T == T_UDT:
                    pe.wait_ge(s["g_done"], b + 1)
                    pe.wait_ge(s["uz_done"], b + 1)
                    stand_alone(pe, b)
                    pe.matmul(front[0:2 * S, :], w_xdt[:, :], uz[:, :],
                              start=True, stop=True).then_inc(s["udt_ps"], 1)
                elif T == T_X1:
                    pe.wait_ge(s["ut_done"], b + 1)
                    pe.wait_ge(s["y_done"], b + 1)
                    pe.wait_ge(s["wog_done"], b + 1)
                    by_tile(front, y, w_out_g[:, :], "out_ps")
                elif T == T_HC0:
                    pe.wait_ge(s["x1_done"], b + 1)
                    pe.wait_ge(s["ln1_hat"], NT * (b + 1))
                    turn4(x_hat[1], front, "hc0_ps")
                elif T == T_R0:
                    ffn_r(0, b, front)
                elif T == T_K0:
                    ffn_k(0, b, front)
                elif T == T_KV0:
                    pe.wait_ge(s["ksq0_done"], b + 1)
                    pe.wait_ge(s["wg0_done"], b + 1)
                    by_tile(front, k_sq[0], wv_g0[:, :], "kv0_ps")
                elif T == T_HC1:
                    pe.wait_ge(s["kv0_done"], b + 1)
                    pe.wait_ge(s["ln2_hat"], NT * (b + 1))
                    turn4(x_hat[2], front, "hc1_ps")
                elif T == T_Q:
                    pe.wait_ge(s["hc1_done"], b + 1)
                    pe.matmul(front[:, :], wq_sb[:, :], h_ch[1][:, 1:],
                              start=True, stop=True).then_inc(s["q_ps"], 1)
                elif T == T_K:
                    pe.wait_ge(s["q_full"], b + 1)
                    pe.matmul(front[:, :], wk_sb[:, :], h_ch[1][:, 1:],
                              start=True, stop=True).then_inc(s["k_ps"], 1)
                elif T == T_V:
                    pe.wait_ge(s["k_full"], b + 1)
                    by_tile(front, h_ch[1][:, 1:], wv_sb[:, :], "v_ps")
                elif T == T_OC:
                    pe.wait_ge(s["o_norm"], NG * (b + 1))
                    turn4(o_tok, end, "oc_ps")
                elif T == T_X3:
                    pe.wait_ge(s["oc_done"], b + 1)
                    pe.wait_ge(s["wog1_done"], b + 1)
                    by_tile(end, o_ch, wo_g[:, q], "wo_ps")
                elif T == T_HC2:
                    pe.wait_ge(s["x3_done"], b + 1)
                    pe.wait_ge(s["ln3_hat"], NT * (b + 1))
                    turn4(x_hat[3], end, "hc2_ps")
                elif T == T_R1:
                    ffn_r(1, b, end)
                elif T == T_K1:
                    ffn_k(1, b, end)
                elif T == T_KV1:
                    pe.wait_ge(s["ksq1_done"], b + 1)
                    pe.wait_ge(s["wg1_done"], b + 1)
                    by_tile(end, k_sq[1], wv_g1[:, q], "kv1_ps")

            iterations(pe, stage)

        @block.vector
        def _(dve):
            nc.vector.memset(y[S:S + 1, :], 1.0).then_inc(s["vec_fill"], 1)
            for n in range(3):
                nc.vector.memset(h_ch[n][:, 0:1], 0.0).then_inc(s["vec_fill"], 1)
            for n in range(2):
                nc.vector.memset(v_aug[:, n, :, :, HD + 1:], 0.0).then_inc(s["vec_fill"], 1)
                nc.vector.memset(v_aug[:, n, :, :, HD:HD + 1], 1.0).then_inc(s["vec_fill"], 1)
            dve.wait_ge(s["c_tanh_done"], 1)
            nc.vector.scalar_tensor_tensor(c_silu[:, :, :], c_tanh[:, :, :], 1.0, c_sb[:, :, :], ALU.add,
                                           ALU.mult).then_inc(s["gate_step"], 1)
            dve.wait_ge(s["gate_step"], 1)
            nc.vector.tensor_scalar(c_silu[:, :, :], c_silu[:, :, :], 0.5, None, ALU.mult)\
                .then_inc(s["c_silu_done"], 1)
            dve.wait_ge(s["modrow_ps"], 1)
            nc.vector.tensor_copy(mod_row[:, 0], row_bank[0][0:NB, 0:D]).then_inc(s["gate_step"], 1)
            nc.vector.tensor_scalar(mod_row[:, 1], row_bank[0][0:NB, D:2 * D], 1.0, None, ALU.add)\
                .then_inc(s["gate_step"], 1)
            for n in range(2):
                nc.vector.tensor_copy(gate_raw[:, 2 * n], row_bank[n][0:NB, 2 * D:3 * D])\
                    .then_inc(s["gate_step"], 1)
                nc.vector.tensor_copy(gate_raw[:, 2 * n + 1], col_bank[n][0:NB, D:2 * D])\
                    .then_inc(s["gate_step"], 1)
            dve.wait_ge(s["gate_step"], 7)
            nc.vector.tensor_scalar(gate_sign, gate_raw, 0.0, 2.0, ALU.is_ge, ALU.mult)\
                .then_inc(s["gate_step"], 1)
            dve.wait_ge(s["gate_step"], 8)
            nc.vector.scalar_tensor_tensor(gate_abs, gate_sign, -1.0, gate_raw, ALU.add, ALU.mult)\
                .then_inc(s["gate_step"], 1)
            dve.wait_ge(s["gate_step"], 9)
            nc.vector.tensor_scalar(gate_size, gate_abs, 0.25, None, ALU.max).then_inc(s["gate_step"], 1)
            dve.wait_ge(s["gate_step"], 10)
            nc.vector.scalar_tensor_tensor(mod_row[:, 2:6], gate_sign, -1.0, gate_size,
                                           ALU.add, ALU.mult).then_inc(s["modrow_done"], 1)
            dve.wait_ge(s["modcol_ps"], 1)
            nc.vector.tensor_scalar(mod_col[:, 0:3], front[:, 0:3 * NB].rearrange("p (k b) -> p k b", k=3),
                                    1.0, None, ALU.add).then_inc(s["gate_step"], 1)
            nc.vector.tensor_copy(mod_col[:, 3:6], front[:, 3 * NB:6 * NB].rearrange("p (k b) -> p k b", k=3))\
                .then_inc(s["mod_ready"], 1)
            nc.vector.tensor_scalar(w_in_sb[:, :], w_in_sb[:, :], w_norm_sb[:, :], None, ALU.mult)\
                .then_inc(s["w_scaled"], 1)
            nc.vector.tensor_scalar(b_uzg[2 * S:3 * S, :], b_uzg[2 * S:3 * S, :], 0.5, None, ALU.mult)\
                .then_inc(s["w_scaled"], 1)
            nc.vector.tensor_scalar(b_xdt[S:2 * S, :], b_xdt[S:2 * S, :], 0.5, None, ALU.mult)\
                .then_inc(s["w_scaled"], 1)
            nc.vector.tensor_scalar(w_out_sb[0:S, :], w_out_sb[0:S, :], 0.25, None, ALU.mult)\
                .then_inc(s["w_scaled"], 1)
            for n in range(2):
                nc.vector.tensor_scalar(ffn_w[:, n, 2], ffn_w[:, n, 2], 0.5, None, ALU.mult)\
                    .then_inc(s["w_scaled"], 1)
            dve.wait_ge(s["w_scaled"], 6)
            dve.wait_ge(s["vec_fill"], 8)
            dve.wait_ge(s["gate_step"], 11)
            dve.wait_ge(s["bias_exp"], 1)
            dve.wait_ge(s["pool_const"], 7)
            dve.sem_inc(s["vec_const"], 1)

            def ln_stats(n, b, src):
                for t in range(NT):
                    nc.vector.bn_stats(stats[n][:, t], src[:, t]).then_inc(s[f"ln{n}_stat"], 1)
                dve.wait_ge(s[f"ln{n}_stat"], NT * (b + 1))
                stand_alone(dve, b)
                for t in range(NT):
                    nc.vector.bn_aggr(mean_var[n][:, t], stats[n][:, t]).then_inc(s[f"ln{n}_mv"], 1)

            def normalize(n, b, src):
                dve.wait_ge(s[f"ln{n}_rs"], 2 * (b + 1))
                for t in range(NT):
                    nc.vector.tensor_scalar(x_hat[n][:, t], src[:, t], mean_var[n][:, t, 0:1],
                                            rstd[n][:, t:t + 1], ALU.subtract,
                                            ALU.mult).then_inc(s[f"ln{n}_hat"], 1)

            def mix(n, b):
                dve.wait_ge(s[f"diff{n}_done"], b + 1)
                nc.vector.scalar_tensor_tensor(mix_r[n], h_diff[n], ffn_mu[:, n, 0:1], h_ch[2 * n][:, 0:L],
                                               ALU.mult, ALU.add).then_inc(s[f"mix{n}_done"], 1)
                nc.vector.scalar_tensor_tensor(mix_k[n], h_diff[n], ffn_mu[:, n, 1:2], h_ch[2 * n][:, 0:L],
                                               ALU.mult, ALU.add).then_inc(s[f"mix{n}_done"], 1)

            def ffn_gate(n, b, src):
                dve.wait_ge(s[f"r{n}_done"], b + 1)
                dve.wait_ge(s[f"kv{n}_ps"], b + 1)
                nc.vector.scalar_tensor_tensor(ffn_out[n][:, :, :], tiles(r_tanh[n][:, :]), 1.0,
                                               tiles(src[:, :]), ALU.add, ALU.mult)\
                    .then_inc(s[f"kv{n}_done"], 1)

            def masked_max(dst, src):
                keys = src.shape[1]
                nc.vector.tensor_tensor_reduce(src, src, mask_row[:, L - keys:], 1.0, LOWEST, ALU.add,
                                               ALU.max, dst).then_inc(s["row_read"], 1)

            def stage(b, q, T):
                g, k = group_at(T, T_ROW)
                if k is not None:
                    G = NG * b + g
                    if k == 0:
                        dve.wait_ge(s["max_split"], floor0(G - 1))
                    dve.wait_ge(s["row_ready"], NU * G + k + 1)
                    stand_alone(dve, G)
                    src, dst = row_bank[k % 2], row_max[:, g % 2]
                    if k < 4:
                        masked_max(dst[:, k, 3:4], src[:, :])
                    elif k < 8:
                        masked_max(dst[:, k - 4, 2:3], src[:, 0:3 * P])
                        masked_max(dst[:, k - 4, 0:1], src[:, 3 * P:])
                    else:
                        masked_max(dst[:, k - 8, 1:2], src[:, 0:2 * P])
                        masked_max(dst[:, k - 6, 1:2], src[:, 2 * P:])
                g, k = group_at(T, T_TURN)
                if k == 2:
                    G = NG * b + g
                    dve.wait_ge(s["turn_ready"], G + 1)
                    heads = turn[:, :].rearrange("p (t h c) -> p t h c", t=NT, h=HG)
                    nc.vector.tensor_tensor(denom[:, :, :], heads[:, :, :, HD],
                                            over(exp_bias[:, HG * g:HG * (g + 1)]), ALU.add)\
                        .then_inc(s["denom_step"], 1)
                    dve.wait_ge(s["denom_step"], 2 * G + 1)
                    nc.vector.reciprocal(denom_inv[:, :, :], denom[:, :, :]).then_inc(s["denom_step"], 1)
                    dve.wait_ge(s["denom_step"], 2 * G + 2)
                    dst = o_tok[:, :, D // NG * g:D // NG * (g + 1)].rearrange("p t (h d) -> p t h d", h=HG)
                    nc.vector.tensor_tensor(dst, heads[:, :, :, 0:HD],
                                            denom_inv[:, :, :].unsqueeze(3).broadcast_to([P, NT, HG, HD]),
                                            ALU.mult).then_inc(s["o_norm"], 1)
                if T == T_LN0:
                    dve.wait_ge(s["x_loaded"], 16 * (b + 1))
                    ln_stats(0, b, x_in[:, q])
                elif T == T_H:
                    normalize(0, b, x_in[:, q])
                elif T == T_RMS:
                    dve.wait_ge(s["h_sq_done"], b + 1)
                    nc.vector.tensor_reduce(h_sum[:, :], h_sq[:, :, :], AX_X, ALU.add)\
                        .then_inc(s["h_sum_done"], 1)
                elif T == T_SCAN:
                    dve.wait_ge(s["dt_done"], b + 1)
                    nc.vector.tensor_scalar(keep[:, :], dt_tanh[:, :], -0.5, 0.5, ALU.mult, ALU.add)\
                        .then_inc(s["scan_step"], 1)
                    dve.wait_ge(s["ut_done"], b + 1)
                    nc.vector.scalar_tensor_tensor(feed[:, :], dt_tanh[:, :], 1.0, u_tanh[:, :], ALU.add,
                                                   ALU.mult).then_inc(s["scan_step"], 1)
                    dve.wait_ge(s["scan_step"], 3 * b + 2)
                    nc.vector.tensor_tensor_scan(state[:, :], keep[:, :], feed[:, :], 0.0, ALU.mult, ALU.add)\
                        .then_inc(s["scan_step"], 1)
                    dve.wait_ge(s["scan_step"], 3 * b + 3)
                    dve.wait_ge(s["g_done"], b + 1)
                    nc.vector.scalar_tensor_tensor(y[0:S, :], g_tanh[:, :], 1.0, state[:, :], ALU.add,
                                                   ALU.mult).then_inc(s["y_done"], 1)
                elif T == T_X1:
                    dve.wait_ge(s["xh_done"], b + 1)
                    dve.wait_ge(s["out_ps"], b + 1)
                    nc.vector.tensor_tensor(x1[:, :, :], x_plus_h[:, :, :], tiles(front[:, :]), ALU.add)\
                        .then_inc(s["x1_done"], 1)
                    dve.wait_ge(s["x1_done"], b + 1)
                    ln_stats(1, b, x1)
                elif T == T_HAT1:
                    normalize(1, b, x1)
                elif T == T_MIX0:
                    mix(0, b)
                elif T == T_KV0:
                    ffn_gate(0, b, front)
                elif T == T_LN2:
                    dve.wait_ge(s["x2_done"], b + 1)
                    ln_stats(2, b, x2)
                elif T == T_HAT2:
                    normalize(2, b, x2)
                elif T == T_X3:
                    dve.wait_ge(s["x4_done"], b)
                    dve.wait_ge(s["xbo_done"], b + 1)
                    dve.wait_ge(s["wo_ps"], b + 1)
                    nc.vector.tensor_tensor(x3[:, :, :], x_bo[:, q], tiles(end[:, :]), ALU.add)\
                        .then_inc(s["x3_done"], 1)
                    dve.wait_ge(s["x3_done"], b + 1)
                    ln_stats(3, b, x3)
                elif T == T_HAT3:
                    normalize(3, b, x3)
                elif T == T_MIX1:
                    mix(1, b)
                elif T == T_KV1:
                    ffn_gate(1, b, end)

            iterations(dve, stage)


N_WEIGHTS = 4 + 9 + 4 + 2 + 2 * 5

_INS = ["L0_attn_x", "L0_attn_W_in", "L0_attn_w_norm", "L0_attn_b_in", "L0_attn_W_x", "L0_attn_b_x",
        "L0_attn_W_dt", "L0_attn_b_dt", "L0_attn_W_out", "L0_attn_b_out"]
_FFN = ["W_r", "W_k", "W_v", "mu_r", "mu_k"]
_TURNED = ("W_r", "W_k", "W_v", "Wq", "Wk", "Wv", "Wo", "_c")


def kernel(**inputs):
    import numpy as _np
    import concourse.bacc as _bacc
    from concourse import mybir as _mybir
    from concourse.bass_utils import run_bass_kernel_spmd as _run

    nc = _bacc.Bacc("TRN2", target_bir_lowering=False, num_devices=1)
    arrays = {}

    def give(name):
        a = _np.asarray(inputs[name])
        if name.endswith(("Wq", "Wk")):
            a = a.reshape(H, HD, D).transpose(1, 0, 2).reshape(D, D)
        if name.endswith(_TURNED):
            a = a.T
        a = _np.ascontiguousarray(a)
        arrays[f"in_{name}"] = a
        return nc.dram_tensor(f"in_{name}", a.shape, _mybir.dt.from_np(a.dtype), kind="ExternalInput").ap()

    layer0 = [give(n) for n in _INS]
    f0 = [give(f"L0_ffn_{n}") for n in _FFN]
    c0, wmod0 = give("L0_c"), give("L0_wmod")
    attn = [give(f"L1_attn_{n}") for n in ("Wq", "Wk", "Wv", "Wo", "bo", "denom_bias")]
    f1 = [give(f"L1_ffn_{n}") for n in _FFN]
    c1, wmod1 = give("L1_c"), give("L1_wmod")
    out = nc.dram_tensor("out", (NB, L, D), F32, kind="ExternalOutput").ap()
    build(nc, *layer0, f0, c0, wmod0, *attn, f1, c1, wmod1, out)
    r = _run(nc, [arrays], core_ids=[0])
    return r.results[0]["out"]
```

```python
from contextlib import ExitStack

import concourse.bass as bass
from concourse import mybir

ALU = mybir.AluOpType
ACT = mybir.ActivationFunctionType
AX_X = mybir.AxisListType.X
F32 = mybir.dt.float32
BF16 = mybir.dt.bfloat16

NB = 8
L = 512
D = 128
P = 128
NT = L // P
S = 32
H = 16
HD = D // H
HG = 4
NG = H // HG
NU = 10
HALF = 64
PARTS = 3
NS = PARTS * (PARTS + 1) // 2
KA = NS * HD
KB = KA + PARTS
NEG = -1.0e30
LOWEST = -3.0e38
LN_EPS = 1e-5
RMS_EPS = 1e-8
LOADS = 2 * (PARTS + 1)
READS = (1, 2, 3, 4, 6, 8, 10, 12, 14, 16)
NR = READS[-1]

WEIGH = ((0, 0, 256), (0, 256, 512), (1, 128, 320), (1, 320, 512), (2, 256, 512), (3, 384, 512))

PERIOD = NG * NU
DEPTH = 5
T_LOAD = 0
T_LN0 = 5
T_STD0 = 7
T_HAT0 = 12
T_MOD = 25
T_H = 29
T_SQ = 33
T_SUM = 35
T_RMS = 36
T_XH = 50
T_HN = 42
T_GATE0 = 43
T_UZG = 44
T_UDT = 47
T_SCAN = 49
T_X1 = 53
T_LN1 = 55
T_STD1 = 57
T_HAT1 = 60
T_HC0 = 61
T_DIFF0 = 62
T_MIX0 = 64
T_R0 = 66
T_K0 = 68
T_KV0 = 70
T_X2 = 71
T_LN2 = 73
T_STD2 = 75
T_HAT2 = 76
T_HC1 = 79
T_Q = 80
T_K = 81
T_REST_Q = 81
T_REST_K = 83
T_PART2_Q = 83
T_PART2_K = 85
T_PART3_Q = 84
T_PART3_K = 86
T_V = 90
T_STORE_Q = 85
T_STACK_Q = 87
T_STORE_K = 88
T_STACK_K = 92
T_GATE1 = 104
T_ROW = 98
T_MAX = T_ROW + NU
T_COL = T_ROW + 2 * NU
T_PV = T_COL + NU + 1
T_TURN = T_PV + len(WEIGH)
T_LOAD_GB = T_TURN + NU * (NG - 1)
T_OC = T_TURN + NU * (NG - 1) + 8
T_X3 = T_OC + 7
T_LN3 = T_X3 + 2
T_STD3 = T_X3 + 4
T_GATE2 = T_X3 + 8
T_HAT3 = T_X3 + 6
T_HC2 = T_X3 + 8
T_DIFF1 = T_X3 + 9
T_MIX1 = T_X3 + 11
T_R1 = T_X3 + 13
T_K1 = T_X3 + 15
T_KV1 = T_X3 + 18
T_OUT = T_X3 + 19
assert T_OUT < PERIOD * DEPTH


def build(nc, x, w_in, w_norm, b_in, w_x, b_x, w_dt, b_dt, w_out, b_out, f0, c0T, wmod0,
          wqT, wkT, wvT, woT, bo, denom_bias, f1, c1T, wmod1, out):
    ctx = ExitStack()
    with ctx:
        def sb(name, shape, dt=F32):
            return ctx.enter_context(nc.sbuf_tensor(name, shape, dt))

        def bank(name):
            return ctx.enter_context(nc.psum_tensor(name, [P, 512], F32))

        mod_dram = nc.dram_tensor("mod_rows", (NB, 6 * D), F32).ap()
        q_dram = nc.dram_tensor("q_parts", (2, PARTS, HD, H, L), BF16).ap()
        k_dram = nc.dram_tensor("k_parts", (2, NS, HD, H, L), BF16).ap()

        ident = sb("ident", [P, P])
        identb = sb("identb", [P, P], BF16)
        mask_row = sb("mask_row", [P, L], BF16)
        mask_col = sb("mask_col", [P, 2, P], BF16)
        neg_half = sb("neg_half", [P, NT])
        w_in_sb = sb("w_in_sb", [P, 3 * S])
        w_norm_sb = sb("w_norm_sb", [P, 1])
        b_uzg = sb("b_uzg", [3 * S, 1])
        w_xdt = sb("w_xdt", [2 * S, 2 * S])
        b_xdt = sb("b_xdt", [2 * S, 1])
        w_out_sb = sb("w_out_sb", [S + 1, D])
        c_sb = sb("c_sb", [P, 2, NB])
        c_tanh = sb("c_tanh", [P, 2, NB])
        c_silu = sb("c_silu", [P, 2, NB])
        wmod_sb = sb("wmod_sb", [P, 2, 6 * D])
        mod_col = sb("mod_col", [P, 6, NB])
        mod_row = sb("mod_row", [NB, 6, D])
        wq_sb = sb("wq_sb", [P, D])
        wk_sb = sb("wk_sb", [P, D])
        wv_sb = sb("wv_sb", [P, D])
        wo_sb = sb("wo_sb", [P, D])
        bo_sb = sb("bo_sb", [P, D])
        exp_bias = sb("exp_bias", [P, H])
        ffn_w = sb("ffn_w", [P, 2, 3, D])
        ffn_mu = sb("ffn_mu", [P, 2, 2])

        mod = sb("mod", [P, 2, 5, D])
        gb1 = sb("gb1", [P, D])
        x_in = sb("x_in", [P, 2, NT, D])
        stats = [sb(f"stats{n}", [P, NT, 6]) for n in range(4)]
        mean_var = [sb(f"mean_var{n}", [P, NT, 2]) for n in range(4)]
        var_eps = [sb(f"var_eps{n}", [P, NT]) for n in range(4)]
        rstd = [sb(f"rstd{n}", [P, NT]) for n in range(4)]
        x_hat = [sb(f"x_hat{n}", [P, NT, D]) for n in range(4)]
        h_tok = sb("h_tok", [P, NT, D])
        h_sq = sb("h_sq", [P, NT, D])
        h_sum = sb("h_sum", [P, NT])
        h_mean = sb("h_mean", [P, NT])
        h_rms = sb("h_rms", [P, NT])
        h_norm = h_sq
        hn_ch = sb("hn_ch", [P, L])
        w_out_g = sb("w_out_g", [S + 1, D])
        g_tanh = sb("g_tanh", [S, L])
        uz = sb("uz", [2 * S, L])
        u_tanh = sb("u_tanh", [S, L])
        dt_tanh = sb("dt_tanh", [S, L])
        keep = sb("keep", [S, L])
        feed = sb("feed", [S, L])
        state = sb("state", [S, L])
        y = sb("y", [S + 1, L])
        gate_raw, gate_sign, gate_abs, gate_size = (t[0:NB, :].rearrange("b (k c) -> b k c", k=4)
                                                    for t in (keep, feed, state, u_tanh))
        x1 = sb("x1", [P, NT, D])
        x2 = sb("x2", [P, NT, D])
        x_bo = sb("x_bo", [P, 2, NT, D])
        g_bo = sb("g_bo", [P, D])
        x3 = sb("x3", [P, NT, D])
        x4 = sb("x4", [P, NT, D])
        wo_g = sb("wo_g", [P, 2, D])
        wv_g0 = sb("wv_g0", [P, D])
        wv_g1 = sb("wv_g1", [P, D])
        h_ch = [sb(f"h_ch{n}", [P, 1 + L]) for n in range(3)]
        h_diff = [x_hat[1][:, :, :].rearrange("p t c -> p (t c)"), x_hat[3][:, :, :].rearrange("p t c -> p (t c)")]
        mix_k = h_diff
        ffn_out = [sb(f"ffn_out{n}", [P, NT, D]) for n in range(2)]
        mix_r = [t[:, :, :].rearrange("p t c -> p (t c)") for t in ffn_out]
        r_tanh = [sb(f"r_tanh{n}", [P, L]) for n in range(2)]
        k_sq = [sb(f"k_sq{n}", [P, L]) for n in range(2)]
        qk_full = sb("qk_full", [P, 2, L])
        qk_rest = sb("qk_rest", [P, 2, L])
        qk_part = sb("qk_part", [P, 2, PARTS, L], BF16)
        q_stack = sb("q_stack", [P, 2, H // 2, L], BF16)
        k_stack = sb("k_stack", [P, 2, H // 2, L], BF16)
        v_aug = sb("v_aug", [P, 2, NT, H, 32])
        row_max = sb("row_max", [P, 2, HG, NT])
        max_rest = sb("max_rest", [P, HG, NT])
        max_part = sb("max_part", [P, HG, PARTS, NT], BF16)
        max_rows = sb("max_rows", [HG * PARTS * NT, 2, P], BF16)
        probs = sb("probs", [P, 2, NU, 512])
        o_heads = sb("o_heads", [P, L])
        denom = sb("denom", [P, NT, HG])
        denom_inv = sb("denom_inv", [P, NT, HG])
        o_tok = sb("o_tok", [P, NT, D])
        o_ch = sb("o_ch", [P, L])

        row_bank = [bank(f"row_bank{n}") for n in range(2)]
        col_bank = [bank(f"col_bank{n}") for n in range(2)]
        pv_bank = bank("pv_bank")
        front = bank("front")
        end = bank("end")
        turn = bank("turn")
        turn_b = turn[:, :].bitcast(BF16)

        names = """c_loaded w_loaded w_zero pool_zero pool_const vec_const vec_fill c_tanh_done c_silu_done
        modrow_ps modcol_ps mod_ready gate_step modrow_done mod_stored w_scaled bias_exp
        mod_loaded gb1_loaded x_loaded
        ln0_stat ln0_mv ln0_rs ln0_hat ln1_stat ln1_mv ln1_rs ln1_hat
        ln2_stat ln2_mv ln2_rs ln2_hat ln3_stat ln3_mv ln3_rs ln3_hat
        h_scaled h_done h_sq_done h_sum_done rms_step hn_done gh_done xh_done wog_done wg0_done
        hn_ps hn_copied uzg_ps uz_done g_done udt_ps ut_done dt_done
        scan_step y_done out_ps x1_done
        hc0_ps hc0_done diff0_done mix0_done r0_ps r0_done k0_ps k0_done ksq0_done kv0_ps kv0_done x2_done
        hc1_ps hc1_done q_ps q_full k_ps k_full v_ps v_done
        part1_done rest_done part2_done part3_done parts_stored stacks_loaded
        gbo_done xbo_done wog1_done wg1_done
        row_ready row_read max_step max_split max_ps max_copied max_loaded
        col_ready exp_done pv_done o_copied turn_ready denom_step o_norm
        oc_ps oc_done wo_ps x3_done
        hc2_ps hc2_done diff1_done mix1_done r1_ps r1_done k1_ps k1_done ksq1_done kv1_ps kv1_done
        x4_done out_stored waited""".split()
        s = {name: ctx.enter_context(nc.semaphore(name)) for name in names}

        def floor0(count):
            return max(count, 0) if isinstance(count, int) else count

        def stand_alone(eng, count):
            if not isinstance(count, int):
                eng.sem_inc(s["waited"], 1)

        def over(t):
            return t.unsqueeze(1).broadcast_to([t.shape[0], NT, t.shape[1]])

        def along(t):
            return t.unsqueeze(2).broadcast_to([P, NT, D])

        def tiles(t):
            return t.rearrange("p (t c) -> p t c", t=NT)

        def group_at(T, start):
            if 0 <= T - start < PERIOD:
                return (T - start) // NU, (T - start) % NU
            return None, None

        def iterations(eng, stage):
            def body(i, parity):
                for slot in range(PERIOD):
                    for n in range(DEPTH):
                        b = i + 1 - n
                        if not isinstance(b, int) or 0 <= b < NB:
                            stage(b, (parity + 1 - n) % 2, PERIOD * n + slot)

            first, end = DEPTH - 2, NB - 1
            end -= (end - first) % 2
            for i in range(-1, first):
                body(i, i % 2)
            with eng.Fori(first, end - 1, 2) as i:
                body(i, first % 2)
                body(i + 1, (first + 1) % 2)
            for i in range(end, NB + DEPTH - 2):
                body(i, i % 2)

        block = ctx.enter_context(nc.Block())

        @block.sync
        def _(sp):
            def load(dst, src, name):
                sp.dma_start(dst, src).then_inc(s[name], 16)

            def col(v, lo, hi):
                return v[lo:hi].rearrange("(p o) -> p o", o=1)

            def load_x(b, q):
                load(x_in[:, q], x[bass.ds(b, 1)].rearrange("o (t p) c -> p (o t) c", p=P), "x_loaded")

            sp.sem_inc(s["out_stored"], 16)
            load(c_sb[:, 0], c0T, "c_loaded")
            load(c_sb[:, 1], c1T, "c_loaded")
            load(wmod_sb[:, 0], wmod0, "c_loaded")
            load(wmod_sb[:, 1], wmod1, "c_loaded")
            load_x(0, 0)
            load(w_in_sb[:, :], w_in, "w_loaded")
            load(w_norm_sb[:, :], col(w_norm, 0, D), "w_loaded")
            load(b_uzg[:, :], col(b_in, 0, 3 * S), "w_loaded")
            sp.wait_ge(s["w_zero"], 1)
            load(w_xdt[0:S, 0:S], w_x, "w_loaded")
            load(w_xdt[S:2 * S, S:2 * S], w_dt, "w_loaded")
            load(b_xdt[0:S, :], col(b_x, 0, S), "w_loaded")
            load(b_xdt[S:2 * S, :], col(b_dt, 0, S), "w_loaded")
            load(w_out_sb[0:S, :], w_out, "w_loaded")
            load(w_out_sb[S:S + 1, :], b_out.rearrange("(o n) -> o n", o=1), "w_loaded")
            for dst, src in ((wq_sb, wqT), (wk_sb, wkT), (wv_sb, wvT), (wo_sb, woT)):
                load(dst[:, :], src, "w_loaded")
            load(bo_sb[:, :], bo.partition_broadcast(P), "w_loaded")
            load(exp_bias[:, :], denom_bias.rearrange("a h b c -> (a h b c)").partition_broadcast(P), "w_loaded")
            for n, f in enumerate((f0, f1)):
                for j in range(3):
                    load(ffn_w[:, n, j], f[j], "w_loaded")
                for j in range(2):
                    load(ffn_mu[:, n, j:j + 1], col(f[3 + j], 0, D), "w_loaded")
            sp.wait_ge(s["modrow_done"], 1)
            load(mod_dram.rearrange("b (k c) -> b k c", k=6), mod_row[:, :, :], "mod_stored")
            sp.wait_ge(s["mod_stored"], 16)
            sp.wait_ge(s["pool_const"], 7)

            def stage(b, q, T):
                if T == T_LOAD:
                    if not isinstance(b, int) or b > 0:
                        sp.wait_ge(s["x1_done"], floor0(b - 1))
                        stand_alone(sp, b)
                        sp.wait_ge(s["x_loaded"], 16 * b)
                        stand_alone(sp, b)
                        load_x(b, q)
                if T == T_MOD:
                    if not isinstance(b, int) or b > 0:
                        sp.wait_ge(s["mod_loaded"], 16 * b)
                        stand_alone(sp, b)
                    sp.wait_ge(s["wog1_done"], floor0(b - 1))
                    stand_alone(sp, b)
                    row = mod_dram[bass.ds(b, 1), 0:5 * D].rearrange("o n -> (o n)").partition_broadcast(P)
                    load(mod[:, q].rearrange("p k c -> p (k c)"), row, "mod_loaded")
                if T == T_LOAD_GB:
                    row = mod_dram[bass.ds(b, 1), 5 * D:].rearrange("o n -> (o n)").partition_broadcast(P)
                    load(gb1[:, :], row, "gb1_loaded")
                for n, (store, stack) in enumerate(((T_STORE_Q, T_STACK_Q), (T_STORE_K, T_STACK_K))):
                    stores = 16 * (1 + PARTS) * b + 16 * (1, 1 + PARTS)[n]
                    if T == store:
                        for done in ("part1_done", "part2_done", "part3_done"):
                            sp.wait_ge(s[done], 2 * b + n + 1)
                            stand_alone(sp, b)
                    if T == store and n == 0:
                        load(q_dram[q].rearrange("j d h l -> (d h) j l"), qk_part[:, 0], "parts_stored")
                    elif T == store:
                        slot = 0
                        for part in range(PARTS):
                            m = PARTS - part
                            load(k_dram[q, slot:slot + m].rearrange("j d h l -> (d h) j l"),
                                 qk_part[:, 1, part].unsqueeze(1).broadcast_to([P, m, L]), "parts_stored")
                            slot += m
                    if T == stack:
                        sp.wait_ge(s["parts_stored"], stores)
                        stand_alone(sp, b)
                    if T == stack and n == 0:
                        sp.wait_ge(s["stacks_loaded"], 16 * LOADS * b)
                        stand_alone(sp, b)
                        sp.wait_ge(s["col_ready"], floor0(NU * NG * (b - 1)))
                        stand_alone(sp, b)
                        for half in range(2):
                            row = HALF * half
                            for m in range(PARTS, 0, -1):
                                load(q_stack[row:row + HD * m, q],
                                     q_dram[q, 0:m].rearrange("j d (t s) l -> s (j d) t l", s=2)[half],
                                     "stacks_loaded")
                                row += HD * m
                    elif T == stack:
                        for half in range(2):
                            load(k_stack[HALF * half:HALF * half + KA, q],
                                 k_dram[q].rearrange("j d (t s) l -> s (j d) t l", s=2)[half],
                                 "stacks_loaded")
                g, k = group_at(T, T_MAX)
                if k == 3:
                    G = NG * b + g
                    sp.wait_ge(s["max_loaded"], 16 * HG * G)
                    stand_alone(sp, G)
                    sp.wait_ge(s["max_copied"], G + 1)
                    stand_alone(sp, G)
                    for head in range(HG):
                        t, half = 2 * g + head // 2, head % 2
                        n = PARTS * NT * head
                        load(q_stack[HALF * half + KA:HALF * half + KB, q, t, :],
                             max_rows[n:n + PARTS * NT, g % 2, :], "max_loaded")
                if T == T_OUT:
                    sp.wait_ge(s["x4_done"], b + 1)
                    stand_alone(sp, b)
                    dst = out[bass.ds(b, 1)].rearrange("o (t p) c -> p (o t) c", p=P)
                    load(dst, x4[:, :, :], "out_stored")

            iterations(sp, stage)
            sp.wait_ge(s["out_stored"], 16 * (NB + 1))

        @block.gpsimd
        def _(pool):
            nc.gpsimd.memset(w_xdt[:, :], 0.0).then_inc(s["w_zero"], 1)
            nc.gpsimd.memset(ident[:, :], 0.0).then_inc(s["pool_zero"], 1)
            nc.gpsimd.memset(identb[:, :], 0.0).then_inc(s["pool_zero"], 1)
            nc.gpsimd.memset(mask_row[:, :], 0.0).then_inc(s["pool_zero"], 1)
            nc.gpsimd.memset(mask_col[:, :, :], 0.0).then_inc(s["pool_zero"], 1)
            pool.wait_ge(s["pool_zero"], 4)
            for m in (ident, identb):
                nc.gpsimd.affine_select(m[:, :], m[:, :], [[-1, P]], ALU.not_equal, 1.0, base=0,
                                        channel_multiplier=1).then_inc(s["pool_const"], 1)
            nc.gpsimd.affine_select(mask_row[:, L - P:], mask_row[:, L - P:], [[-1, P]], ALU.is_ge, NEG,
                                    base=0, channel_multiplier=1).then_inc(s["pool_const"], 1)
            nc.gpsimd.affine_select(mask_col[:, :, :], mask_col[:, :, :], [[0, 2], [1, P]], ALU.is_ge, NEG,
                                    base=0, channel_multiplier=-1).then_inc(s["pool_const"], 1)
            nc.gpsimd.memset(neg_half[:, :], -0.5).then_inc(s["pool_const"], 1)
            nc.gpsimd.memset(k_stack[:, 0], -1.0).then_inc(s["pool_const"], 1)
            nc.gpsimd.memset(k_stack[:, 1], -1.0).then_inc(s["pool_const"], 1)
            pool.wait_ge(s["pool_const"], 7)

            def inv_std(n, b):
                pool.wait_ge(s[f"ln{n}_mv"], NT * (b + 1))
                stand_alone(pool, b)
                nc.gpsimd.tensor_scalar(var_eps[n][:, :], mean_var[n][:, :, 1], LN_EPS, None,
                                        ALU.add).then_inc(s[f"ln{n}_rs"], 1)
                pool.wait_ge(s[f"ln{n}_rs"], 2 * b + 1)
                stand_alone(pool, b)
                nc.gpsimd.tensor_tensor(rstd[n][:, :], var_eps[n][:, :], neg_half[:, :],
                                        ALU.pow).then_inc(s[f"ln{n}_rs"], 1)

            def diff(n, b):
                pool.wait_ge(s[f"hc{2 * n}_done"], b + 1)
                stand_alone(pool, b)
                nc.gpsimd.tensor_tensor(h_diff[n], h_ch[2 * n][:, 1:1 + L], h_ch[2 * n][:, 0:L],
                                        ALU.subtract).then_inc(s[f"diff{n}_done"], 1)

            def rest(n, b):
                pool.wait_ge(s["part1_done"], 2 * b + n + 1)
                stand_alone(pool, b)
                nc.gpsimd.tensor_tensor(qk_rest[:, n], qk_full[:, n], qk_part[:, n, 0],
                                        ALU.subtract).then_inc(s["rest_done"], 1)

            def last_part(n, b):
                pool.wait_ge(s["part2_done"], 2 * b + n + 1)
                stand_alone(pool, b)
                nc.gpsimd.tensor_tensor(qk_part[:, n, 2], qk_rest[:, n], qk_part[:, n, 1],
                                        ALU.subtract).then_inc(s["part3_done"], 1)

            def max_parts(G, gp):
                pool.wait_ge(s["row_read"], NR * (G + 1))
                stand_alone(pool, G)
                pool.wait_ge(s["max_ps"], G)
                stand_alone(pool, G)
                full = row_max[:, gp]
                nc.gpsimd.tensor_copy(max_part[:, :, 0, :], full).then_inc(s["max_step"], 1)
                pool.wait_ge(s["max_step"], 3 * G + 1)
                stand_alone(pool, G)
                nc.gpsimd.tensor_tensor(max_rest[:, :, :], full, max_part[:, :, 0, :],
                                        ALU.subtract).then_inc(s["max_step"], 1)
                pool.wait_ge(s["max_step"], 3 * G + 2)
                stand_alone(pool, G)
                nc.gpsimd.tensor_copy(max_part[:, :, 1, :], max_rest[:, :, :]).then_inc(s["max_step"], 1)
                pool.wait_ge(s["max_step"], 3 * G + 3)
                stand_alone(pool, G)
                nc.gpsimd.tensor_tensor(max_part[:, :, 2, :], max_rest[:, :, :], max_part[:, :, 1, :],
                                        ALU.subtract).then_inc(s["max_split"], 1)

            pool.wait_ge(s["vec_const"], 1)

            def stage(b, q, T):
                g, k = group_at(T, T_MAX)
                if k == 0:
                    max_parts(NG * b + g, g % 2)
                for n, std in enumerate((T_STD0, T_STD1, T_STD2, T_STD3)):
                    if T == std:
                        inv_std(n, b)
                if T == T_H:
                    pool.wait_ge(s["ln0_hat"], NT * (b + 1))
                    stand_alone(pool, b)
                    pool.wait_ge(s["mod_loaded"], 16 * (b + 1))
                    stand_alone(pool, b)
                    nc.gpsimd.tensor_tensor(x_hat[0][:, :, :], x_hat[0][:, :, :], over(mod[:, q, 1]),
                                            ALU.mult).then_inc(s["h_scaled"], 1)
                    pool.wait_ge(s["h_scaled"], b + 1)
                    stand_alone(pool, b)
                    nc.gpsimd.tensor_tensor(h_tok[:, :, :], x_hat[0][:, :, :], over(mod[:, q, 0]),
                                            ALU.add).then_inc(s["h_done"], 1)
                elif T == T_RMS:
                    pool.wait_ge(s["h_sum_done"], b + 1)
                    stand_alone(pool, b)
                    nc.gpsimd.tensor_scalar(h_mean[:, :], h_sum[:, :], 1.0 / D, RMS_EPS, ALU.mult,
                                            ALU.add).then_inc(s["rms_step"], 1)
                    pool.wait_ge(s["rms_step"], 2 * b + 1)
                    stand_alone(pool, b)
                    nc.gpsimd.tensor_tensor(h_rms[:, :], h_mean[:, :], neg_half[:, :],
                                            ALU.pow).then_inc(s["rms_step"], 1)
                    pool.wait_ge(s["rms_step"], 2 * b + 2)
                    stand_alone(pool, b)
                    nc.gpsimd.tensor_tensor(h_norm[:, :, :], h_tok[:, :, :], along(h_rms[:, :]),
                                            ALU.mult).then_inc(s["hn_done"], 1)
                elif T == T_XH:
                    nc.gpsimd.tensor_tensor(h_tok[:, :, :], h_tok[:, :, :], over(mod[:, q, 2]),
                                            ALU.mult).then_inc(s["gh_done"], 1)
                    pool.wait_ge(s["gh_done"], b + 1)
                    stand_alone(pool, b)
                    nc.gpsimd.tensor_tensor(x_in[:, q], h_tok[:, :, :], x_in[:, q],
                                            ALU.add).then_inc(s["xh_done"], 1)
                elif T == T_GATE0:
                    nc.gpsimd.tensor_tensor(w_out_g[:, :], w_out_sb[:, :], mod[0:S + 1, q, 2],
                                            ALU.mult).then_inc(s["wog_done"], 1)
                    nc.gpsimd.tensor_tensor(wv_g0[:, :], ffn_w[:, 0, 2], mod[:, q, 3],
                                            ALU.mult).then_inc(s["wg0_done"], 1)
                elif T == T_DIFF0:
                    diff(0, b)
                elif T == T_X2:
                    pool.wait_ge(s["kv0_done"], b + 1)
                    stand_alone(pool, b)
                    nc.gpsimd.tensor_tensor(x2[:, :, :], x1[:, :, :], ffn_out[0][:, :, :],
                                            ALU.add).then_inc(s["x2_done"], 1)
                if T == T_REST_Q:
                    rest(0, b)
                if T == T_REST_K:
                    rest(1, b)
                if T == T_PART3_Q:
                    last_part(0, b)
                if T == T_PART3_K:
                    last_part(1, b)
                if T == T_GATE1:
                    pool.wait_ge(s["x3_done"], floor0(b - 1))
                    stand_alone(pool, b)
                    pool.wait_ge(s["x2_done"], b + 1)
                    stand_alone(pool, b)
                    nc.gpsimd.tensor_tensor(g_bo[:, :], bo_sb[:, :], mod[:, q, 4],
                                            ALU.mult).then_inc(s["gbo_done"], 1)
                    pool.wait_ge(s["gbo_done"], b + 1)
                    stand_alone(pool, b)
                    nc.gpsimd.tensor_tensor(x_bo[:, q], x2[:, :, :], over(g_bo[:, :]),
                                            ALU.add).then_inc(s["xbo_done"], 1)
                    nc.gpsimd.tensor_tensor(wo_g[:, q], wo_sb[:, :], mod[:, q, 4],
                                            ALU.mult).then_inc(s["wog1_done"], 1)
                elif T == T_GATE2:
                    pool.wait_ge(s["gb1_loaded"], 16 * (b + 1))
                    stand_alone(pool, b)
                    nc.gpsimd.tensor_tensor(wv_g1[:, :], ffn_w[:, 1, 2], gb1[:, :],
                                            ALU.mult).then_inc(s["wg1_done"], 1)
                elif T == T_DIFF1:
                    diff(1, b)
                elif T == T_OUT:
                    pool.wait_ge(s["kv1_done"], b + 1)
                    stand_alone(pool, b)
                    pool.wait_ge(s["out_stored"], 16 * (b + 1))
                    stand_alone(pool, b)
                    nc.gpsimd.tensor_tensor(x4[:, :, :], x3[:, :, :], ffn_out[1][:, :, :],
                                            ALU.add).then_inc(s["x4_done"], 1)

            iterations(pool, stage)

        @block.scalar
        def _(act):
            act.wait_ge(s["c_loaded"], 16 * 4)
            nc.scalar.activation(c_tanh[:, :, :], c_sb[:, :, :], ACT.Tanh, scale=0.5).then_inc(s["c_tanh_done"], 1)
            act.wait_ge(s["w_loaded"], 16 * N_WEIGHTS)
            nc.scalar.activation(exp_bias[:, :], exp_bias[:, :], ACT.Exp).then_inc(s["bias_exp"], 1)
            act.wait_ge(s["vec_const"], 1)
            act.wait_ge(s["mod_ready"], 1)

            def to_channels(n, b, src):
                act.wait_ge(s[f"hc{n}_ps"], b + 1)
                nc.scalar.activation(h_ch[n][:, 1:1 + L], src[:, :], ACT.Identity,
                                     scale=mod_col[:, n, bass.ds(b, 1)],
                                     bias=mod_col[:, n + 3, bass.ds(b, 1)]).then_inc(s[f"hc{n}_done"], 1)

            def ffn_r(n, b, src):
                act.wait_ge(s[f"r{n}_ps"], b + 1)
                nc.scalar.activation(r_tanh[n][:, :], src[:, :], ACT.Tanh, scale=0.5)\
                    .then_inc(s[f"r{n}_done"], 1)

            def ffn_k(n, b, src):
                act.wait_ge(s[f"k{n}_ps"], b + 1)
                nc.scalar.activation(k_sq[n][:, :], src[:, :], ACT.Relu).then_inc(s[f"k{n}_done"], 1)
                act.wait_ge(s[f"k{n}_done"], b + 1)
                nc.scalar.activation(k_sq[n][:, :], k_sq[n][:, :], ACT.Square).then_inc(s[f"ksq{n}_done"], 1)

            def first_part(n, b):
                act.wait_ge(s[("q_full", "k_full")[n]], b + 1)
                nc.scalar.activation(qk_part[:, n, 0], qk_full[:, n], ACT.Copy).then_inc(s["part1_done"], 1)

            def second_part(n, b):
                act.wait_ge(s["rest_done"], 2 * b + n + 1)
                nc.scalar.activation(qk_part[:, n, 1], qk_rest[:, n], ACT.Copy).then_inc(s["part2_done"], 1)

            def stage(b, q, T):
                g, k = group_at(T, T_COL)
                if k is not None:
                    G = NG * b + g
                    if k == 0:
                        act.wait_ge(s["pv_done"], floor0(G - 1))
                    act.wait_ge(s["col_ready"], NU * G + k + 1)
                    nc.scalar.activation(probs[:, g % 2, k], col_bank[k % 2][:, :], ACT.Exp)\
                        .then_inc(s["exp_done"], 1)
                if T == T_SQ:
                    act.wait_ge(s["h_done"], b + 1)
                    nc.scalar.activation(h_sq[:, :, :], h_tok[:, :, :], ACT.Square).then_inc(s["h_sq_done"], 1)
                elif T == T_HN:
                    act.wait_ge(s["hn_ps"], b + 1)
                    nc.scalar.activation(hn_ch[:, :], front[:, :], ACT.Copy).then_inc(s["hn_copied"], 1)
                elif T == T_UZG:
                    act.wait_ge(s["uzg_ps"], b + 1)
                    nc.scalar.activation(uz[:, :], front[0:2 * S, :], ACT.Identity, bias=b_uzg[0:2 * S, :])\
                        .then_inc(s["uz_done"], 1)
                    nc.scalar.activation(g_tanh[:, :], front[2 * S:3 * S, :], ACT.Tanh, scale=0.5,
                                         bias=b_uzg[2 * S:3 * S, :]).then_inc(s["g_done"], 1)
                elif T == T_UDT:
                    act.wait_ge(s["udt_ps"], b + 1)
                    nc.scalar.activation(dt_tanh[:, :], front[S:2 * S, :], ACT.Tanh, scale=0.5,
                                         bias=b_xdt[S:2 * S, :]).then_inc(s["dt_done"], 1)
                    nc.scalar.activation(u_tanh[:, :], front[0:S, :], ACT.Tanh, bias=b_xdt[0:S, :])\
                        .then_inc(s["ut_done"], 1)
                elif T == T_HC0:
                    to_channels(0, b, front)
                elif T == T_R0:
                    ffn_r(0, b, front)
                elif T == T_K0:
                    ffn_k(0, b, front)
                elif T == T_HC1:
                    to_channels(1, b, front)
                elif T == T_Q:
                    act.wait_ge(s["q_ps"], b + 1)
                    nc.scalar.activation(qk_full[:, 0], front[:, :], ACT.Copy, scale=HD ** -0.5)\
                        .then_inc(s["q_full"], 1)
                    first_part(0, b)
                elif T == T_K:
                    act.wait_ge(s["k_ps"], b + 1)
                    nc.scalar.activation(qk_full[:, 1], front[:, :], ACT.Copy).then_inc(s["k_full"], 1)
                    first_part(1, b)
                elif T == T_V:
                    act.wait_ge(s["pv_done"], floor0(NG * (b - 1)))
                    act.wait_ge(s["v_ps"], b + 1)
                    nc.scalar.activation(v_aug[:, q, :, :, 0:HD],
                                         end[:, :].rearrange("p (t h d) -> p t h d", t=NT, h=H),
                                         ACT.Copy).then_inc(s["v_done"], 1)
                elif T == T_OC:
                    act.wait_ge(s["oc_ps"], b + 1)
                    nc.scalar.activation(o_ch[:, :], end[:, :], ACT.Copy).then_inc(s["oc_done"], 1)
                elif T == T_HC2:
                    to_channels(2, b, end)
                elif T == T_R1:
                    ffn_r(1, b, end)
                elif T == T_K1:
                    ffn_k(1, b, end)
                if T == T_PART2_Q:
                    second_part(0, b)
                if T == T_PART2_K:
                    second_part(1, b)
                g, k = group_at(T, T_MAX)
                if k == 3:
                    G = NG * b + g
                    act.wait_ge(s["max_loaded"], floor0(16 * HG * (G - 1)))
                    act.wait_ge(s["max_ps"], G + 1)
                    nc.scalar.activation(max_rows[:, g % 2], turn_b[0:HG * PARTS * NT, 0:P],
                                         ACT.Copy).then_inc(s["max_copied"], 1)
                g, k = group_at(T, T_TURN)
                if k == 0:
                    G = NG * b + g
                    act.wait_ge(s["turn_ready"], G)
                    act.wait_ge(s["pv_done"], G + 1)
                    nc.scalar.activation(o_heads[:, :], pv_bank[:, :], ACT.Copy).then_inc(s["o_copied"], 1)

            iterations(act, stage)

        @block.tensor
        def _(pe):
            def turn4(src, dst, done):
                for t in range(NT):
                    mm = pe.transpose(dst[:, P * t:P * (t + 1)], src[:, t], ident[:, :])
                mm.then_inc(s[done], 1)

            def by_tile(dst, lhs, rhs, done):
                for t in range(NT):
                    mm = pe.matmul(dst[:, P * t:P * (t + 1)], lhs[:, P * t:P * (t + 1)], rhs,
                                   start=True, stop=True)
                mm.then_inc(s[done], 1)

            pe.wait_ge(s["c_silu_done"], 1)
            for n in range(2):
                pe.matmul(row_bank[n][0:NB, :], c_silu[:, n], wmod_sb[:, n, 0:4 * D], start=True, stop=True)
                mm = pe.matmul(col_bank[n][0:NB, 0:2 * D], c_silu[:, n], wmod_sb[:, n, 4 * D:6 * D],
                               start=True, stop=True)
            mm.then_inc(s["modrow_ps"], 1)
            for j, (n, k) in enumerate(((0, 4), (1, 1), (1, 4), (0, 3), (1, 0), (1, 3))):
                mm = pe.matmul(front[:, NB * j:NB * (j + 1)], wmod_sb[:, n, D * k:D * (k + 1)], c_silu[:, n],
                               start=True, stop=True)
            mm.then_inc(s["modcol_ps"], 1)
            pe.wait_ge(s["pool_const"], 7)
            pe.wait_ge(s["vec_const"], 1)
            pe.wait_ge(s["mod_ready"], 1)

            def row_unit(b, q, g, k):
                G = NG * b + g
                read = NR * G + READS[k - 2] if k >= 2 else NR * (G - 1) + READS[NU - 2 + k]
                pe.wait_ge(s["row_read"], floor0(read))
                dst = row_bank[k % 2]

                def scores(c0, t, half, tile, start, stop):
                    rows = slice(HALF * half, HALF * half + KA)
                    return pe.matmul(dst[:, c0:c0 + P * (tile + 1)],
                                     q_stack[rows, q, t, P * tile:P * (tile + 1)],
                                     k_stack[rows, q, t, 0:P * (tile + 1)], start=start, stop=stop,
                                     skip_group_check=True)

                if k < 4:
                    mm = scores(0, 2 * g + k // 2, k % 2, 3, True, True)
                elif k < 8:
                    scores(0, 2 * g + (k - 4) // 2, k % 2, 2, True, False)
                    mm = scores(3 * P, 2 * g + (k - 4) // 2, k % 2, 0, False, True)
                else:
                    scores(0, 2 * g, k - 8, 1, True, False)
                    mm = scores(2 * P, 2 * g + 1, k - 8, 1, False, True)
                mm.then_inc(s["row_ready"], 1)

            def col_unit(b, q, g, k):
                G = NG * b + g
                if k == 0:
                    pe.wait_ge(s["max_loaded"], 16 * HG * (G + 1))
                pe.wait_ge(s["exp_done"], floor0(NU * G + k - 1))
                dst = col_bank[k % 2]

                def scores(c0, t, half, tile, start):
                    rows = slice(HALF * half, HALF * half + KB)
                    pe.matmul(dst[:, c0:c0 + L - P * tile], k_stack[rows, q, t, P * tile:P * (tile + 1)],
                              q_stack[rows, q, t, P * tile:L], start=start, stop=False,
                              skip_group_check=True)

                def mask(c0, m, stop):
                    return pe.matmul(dst[:, c0:c0 + P * m], identb[:, :],
                                     mask_col[:, 0:m, :].rearrange("p m c -> p (m c)"),
                                     start=False, stop=stop, skip_group_check=True)

                if k < 4:
                    scores(0, 2 * g + k // 2, k % 2, 0, True)
                    mm = mask(0, 1, True)
                elif k < 8:
                    scores(0, 2 * g + (k - 4) // 2, k % 2, 3, True)
                    scores(P, 2 * g + (k - 4) // 2, k % 2, 1, False)
                    mm = mask(0, 2, True)
                else:
                    scores(0, 2 * g, k - 8, 2, True)
                    scores(2 * P, 2 * g + 1, k - 8, 2, False)
                    mask(0, 1, False)
                    mm = mask(2 * P, 1, True)
                mm.then_inc(s["col_ready"], 1)

            def weigh(b, q, g, k):
                G = NG * b + g
                tile, lo, hi = WEIGH[k]
                if k == 0:
                    pe.wait_ge(s["o_copied"], G)
                    pe.wait_ge(s["exp_done"], NU * (G + 1))
                for head in range(HG):
                    unit, at = ((head, 0), (4 + head, 0), (8 + head % 2, 2 * P * (head // 2) - 2 * P),
                                (4 + head, -3 * P))[tile]
                    mm = pe.matmul(pv_bank[32 * head:32 * (head + 1), lo:hi],
                                   v_aug[:, q, tile, HG * g + head, :],
                                   probs[:, g % 2, unit, at + lo:at + hi],
                                   start=(k == 0), stop=(k == len(WEIGH) - 1), skip_group_check=True)
                if k == len(WEIGH) - 1:
                    mm.then_inc(s["pv_done"], 1)

            def ffn_r(n, b, dst):
                pe.wait_ge(s[f"mix{n}_done"], 2 * b + 1)
                by_tile(dst, mix_r[n], ffn_w[:, n, 0], f"r{n}_ps")

            def ffn_k(n, b, dst):
                pe.wait_ge(s[f"r{n}_done"], b + 1)
                pe.wait_ge(s[f"mix{n}_done"], 2 * (b + 1))
                pe.matmul(dst[:, :], ffn_w[:, n, 1], mix_k[n], start=True, stop=True).then_inc(s[f"k{n}_ps"], 1)

            def stage(b, q, T):
                g, k = group_at(T, T_ROW)
                if k is not None:
                    if T == T_ROW:
                        pe.wait_ge(s["stacks_loaded"], 16 * LOADS * (b + 1))
                    row_unit(b, q, g, k)
                g, k = group_at(T, T_COL)
                if k is not None:
                    col_unit(b, q, g, k)
                g, k = group_at(T, T_MAX)
                if k == 3:
                    G = NG * b + g
                    pe.wait_ge(s["o_norm"], floor0(G - 2))
                    pe.wait_ge(s["max_split"], G + 1)
                    stand_alone(pe, G)
                    pe.transpose(turn_b[0:HG * PARTS * NT, 0:P],
                                 max_part[:, :, :, :].rearrange("p h j t -> p (h j t)"),
                                 identb[:, :]).then_inc(s["max_ps"], 1)
                g, k = group_at(T, T_PV)
                if k is not None and k < len(WEIGH):
                    weigh(b, q, g, k)
                g, k = group_at(T, T_TURN)
                if k == 2:
                    G = NG * b + g
                    pe.wait_ge(s["max_copied"], min(G + 3, NG * NB) if isinstance(G, int) else G + 3)
                    pe.wait_ge(s["o_norm"], G)
                    pe.wait_ge(s["o_copied"], G + 1)
                    turn4(tiles(o_heads[:, :]), turn, "turn_ready")
                if T == T_HN:
                    pe.wait_ge(s["k_full"], b)
                    pe.wait_ge(s["hn_done"], b + 1)
                    turn4(h_norm, front, "hn_ps")
                elif T == T_UZG:
                    pe.wait_ge(s["hn_copied"], b + 1)
                    pe.matmul(front[0:3 * S, :], w_in_sb[:, :], hn_ch[:, :],
                              start=True, stop=True).then_inc(s["uzg_ps"], 1)
                elif T == T_UDT:
                    pe.wait_ge(s["g_done"], b + 1)
                    pe.wait_ge(s["uz_done"], b + 1)
                    stand_alone(pe, b)
                    pe.matmul(front[0:2 * S, :], w_xdt[:, :], uz[:, :],
                              start=True, stop=True).then_inc(s["udt_ps"], 1)
                elif T == T_X1:
                    pe.wait_ge(s["ut_done"], b + 1)
                    pe.wait_ge(s["y_done"], b + 1)
                    pe.wait_ge(s["wog_done"], b + 1)
                    by_tile(front, y, w_out_g[:, :], "out_ps")
                elif T == T_HC0:
                    pe.wait_ge(s["x1_done"], b + 1)
                    pe.wait_ge(s["ln1_hat"], NT * (b + 1))
                    turn4(x_hat[1], front, "hc0_ps")
                elif T == T_R0:
                    ffn_r(0, b, front)
                elif T == T_K0:
                    ffn_k(0, b, front)
                elif T == T_KV0:
                    pe.wait_ge(s["ksq0_done"], b + 1)
                    pe.wait_ge(s["wg0_done"], b + 1)
                    by_tile(front, k_sq[0], wv_g0[:, :], "kv0_ps")
                elif T == T_HC1:
                    pe.wait_ge(s["kv0_done"], b + 1)
                    pe.wait_ge(s["ln2_hat"], NT * (b + 1))
                    turn4(x_hat[2], front, "hc1_ps")
                elif T == T_Q:
                    pe.wait_ge(s["hc1_done"], b + 1)
                    pe.matmul(front[:, :], wq_sb[:, :], h_ch[1][:, 1:],
                              start=True, stop=True).then_inc(s["q_ps"], 1)
                elif T == T_K:
                    pe.wait_ge(s["q_full"], b + 1)
                    pe.matmul(front[:, :], wk_sb[:, :], h_ch[1][:, 1:],
                              start=True, stop=True).then_inc(s["k_ps"], 1)
                elif T == T_V:
                    pe.wait_ge(s["kv1_done"], floor0(b - 2))
                    by_tile(end, h_ch[1][:, 1:], wv_sb[:, :], "v_ps")
                elif T == T_OC:
                    pe.wait_ge(s["v_done"], min(b + 3, NB) if isinstance(b, int) else b + 3)
                    pe.wait_ge(s["o_norm"], NG * (b + 1))
                    turn4(o_tok, end, "oc_ps")
                elif T == T_X3:
                    pe.wait_ge(s["oc_done"], b + 1)
                    pe.wait_ge(s["wog1_done"], b + 1)
                    by_tile(end, o_ch, wo_g[:, q], "wo_ps")
                elif T == T_HC2:
                    pe.wait_ge(s["x3_done"], b + 1)
                    pe.wait_ge(s["ln3_hat"], NT * (b + 1))
                    turn4(x_hat[3], end, "hc2_ps")
                elif T == T_R1:
                    ffn_r(1, b, end)
                elif T == T_K1:
                    ffn_k(1, b, end)
                elif T == T_KV1:
                    pe.wait_ge(s["ksq1_done"], b + 1)
                    pe.wait_ge(s["wg1_done"], b + 1)
                    by_tile(end, k_sq[1], wv_g1[:, :], "kv1_ps")

            iterations(pe, stage)

        @block.vector
        def _(dve):
            nc.vector.memset(y[S:S + 1, :], 1.0).then_inc(s["vec_fill"], 1)
            for n in range(3):
                nc.vector.memset(h_ch[n][:, 0:1], 0.0).then_inc(s["vec_fill"], 1)
            for n in range(2):
                nc.vector.memset(v_aug[:, n, :, :, HD + 1:], 0.0).then_inc(s["vec_fill"], 1)
                nc.vector.memset(v_aug[:, n, :, :, HD:HD + 1], 1.0).then_inc(s["vec_fill"], 1)
            dve.wait_ge(s["c_tanh_done"], 1)
            nc.vector.scalar_tensor_tensor(c_silu[:, :, :], c_tanh[:, :, :], 1.0, c_sb[:, :, :], ALU.add,
                                           ALU.mult).then_inc(s["gate_step"], 1)
            dve.wait_ge(s["gate_step"], 1)
            nc.vector.tensor_scalar(c_silu[:, :, :], c_silu[:, :, :], 0.5, None, ALU.mult)\
                .then_inc(s["c_silu_done"], 1)
            dve.wait_ge(s["modrow_ps"], 1)
            nc.vector.tensor_copy(mod_row[:, 0], row_bank[0][0:NB, 0:D]).then_inc(s["gate_step"], 1)
            nc.vector.tensor_scalar(mod_row[:, 1], row_bank[0][0:NB, D:2 * D], 1.0, None, ALU.add)\
                .then_inc(s["gate_step"], 1)
            for n in range(2):
                nc.vector.tensor_copy(gate_raw[:, 2 * n], row_bank[n][0:NB, 2 * D:3 * D])\
                    .then_inc(s["gate_step"], 1)
                nc.vector.tensor_copy(gate_raw[:, 2 * n + 1], col_bank[n][0:NB, D:2 * D])\
                    .then_inc(s["gate_step"], 1)
            dve.wait_ge(s["gate_step"], 7)
            nc.vector.tensor_scalar(gate_sign, gate_raw, 0.0, 2.0, ALU.is_ge, ALU.mult)\
                .then_inc(s["gate_step"], 1)
            dve.wait_ge(s["gate_step"], 8)
            nc.vector.scalar_tensor_tensor(gate_abs, gate_sign, -1.0, gate_raw, ALU.add, ALU.mult)\
                .then_inc(s["gate_step"], 1)
            dve.wait_ge(s["gate_step"], 9)
            nc.vector.tensor_scalar(gate_size, gate_abs, 0.25, None, ALU.max).then_inc(s["gate_step"], 1)
            dve.wait_ge(s["gate_step"], 10)
            nc.vector.scalar_tensor_tensor(mod_row[:, 2:6], gate_sign, -1.0, gate_size,
                                           ALU.add, ALU.mult).then_inc(s["modrow_done"], 1)
            dve.wait_ge(s["modcol_ps"], 1)
            nc.vector.tensor_scalar(mod_col[:, 0:3], front[:, 0:3 * NB].rearrange("p (k b) -> p k b", k=3),
                                    1.0, None, ALU.add).then_inc(s["gate_step"], 1)
            nc.vector.tensor_copy(mod_col[:, 3:6], front[:, 3 * NB:6 * NB].rearrange("p (k b) -> p k b", k=3))\
                .then_inc(s["mod_ready"], 1)
            dve.wait_ge(s["w_loaded"], 16 * N_WEIGHTS)
            nc.vector.tensor_scalar(w_in_sb[:, :], w_in_sb[:, :], w_norm_sb[:, :], None, ALU.mult)\
                .then_inc(s["w_scaled"], 1)
            nc.vector.tensor_scalar(b_uzg[2 * S:3 * S, :], b_uzg[2 * S:3 * S, :], 0.5, None, ALU.mult)\
                .then_inc(s["w_scaled"], 1)
            nc.vector.tensor_scalar(b_xdt[S:2 * S, :], b_xdt[S:2 * S, :], 0.5, None, ALU.mult)\
                .then_inc(s["w_scaled"], 1)
            nc.vector.tensor_scalar(w_out_sb[0:S, :], w_out_sb[0:S, :], 0.25, None, ALU.mult)\
                .then_inc(s["w_scaled"], 1)
            for n in range(2):
                nc.vector.tensor_scalar(ffn_w[:, n, 2], ffn_w[:, n, 2], 0.5, None, ALU.mult)\
                    .then_inc(s["w_scaled"], 1)
            dve.wait_ge(s["w_scaled"], 6)
            dve.wait_ge(s["vec_fill"], 8)
            dve.wait_ge(s["gate_step"], 11)
            dve.wait_ge(s["bias_exp"], 1)
            dve.wait_ge(s["pool_const"], 7)
            dve.sem_inc(s["vec_const"], 1)

            def ln_stats(n, b, src, half):
                for t in range(2 * half, 2 * half + 2):
                    nc.vector.bn_stats(stats[n][:, t], src[:, t]).then_inc(s[f"ln{n}_stat"], 1)
                if half == 0:
                    return
                dve.wait_ge(s[f"ln{n}_stat"], NT * (b + 1))
                stand_alone(dve, b)
                for t in range(NT):
                    nc.vector.bn_aggr(mean_var[n][:, t], stats[n][:, t]).then_inc(s[f"ln{n}_mv"], 1)

            def normalize(n, b, src, half):
                dve.wait_ge(s[f"ln{n}_rs"], 2 * (b + 1))
                for t in range(2 * half, 2 * half + 2):
                    nc.vector.tensor_scalar(x_hat[n][:, t], src[:, t], mean_var[n][:, t, 0:1],
                                            rstd[n][:, t:t + 1], ALU.subtract,
                                            ALU.mult).then_inc(s[f"ln{n}_hat"], 1)

            def mix(n, b, dst, j):
                dve.wait_ge(s[f"diff{n}_done"], b + 1)
                nc.vector.scalar_tensor_tensor(dst[n], h_diff[n], ffn_mu[:, n, j:j + 1], h_ch[2 * n][:, 0:L],
                                               ALU.mult, ALU.add).then_inc(s[f"mix{n}_done"], 1)

            def ffn_gate(n, b, src):
                dve.wait_ge(s[f"r{n}_done"], b + 1)
                dve.wait_ge(s[f"kv{n}_ps"], b + 1)
                nc.vector.scalar_tensor_tensor(ffn_out[n][:, :, :], tiles(r_tanh[n][:, :]), 1.0,
                                               tiles(src[:, :]), ALU.add, ALU.mult)\
                    .then_inc(s[f"kv{n}_done"], 1)

            def masked_max(dst, src):
                keys = src.shape[1]
                nc.vector.tensor_tensor_reduce(src, src, mask_row[:, L - keys:], 1.0, LOWEST, ALU.add,
                                               ALU.max, dst).then_inc(s["row_read"], 1)

            def stage(b, q, T):
                g, k = group_at(T, T_ROW)
                if k is not None:
                    G = NG * b + g
                    if k == 0:
                        dve.wait_ge(s["max_split"], floor0(G - 1))
                    dve.wait_ge(s["row_ready"], NU * G + k + 1)
                    stand_alone(dve, G)
                    src, dst = row_bank[k % 2], row_max[:, g % 2]
                    if k < 4:
                        masked_max(dst[:, k, 3:4], src[:, :])
                    elif k < 8:
                        masked_max(dst[:, k - 4, 2:3], src[:, 0:3 * P])
                        masked_max(dst[:, k - 4, 0:1], src[:, 3 * P:])
                    else:
                        masked_max(dst[:, k - 8, 1:2], src[:, 0:2 * P])
                        masked_max(dst[:, k - 6, 1:2], src[:, 2 * P:])
                g, k = group_at(T, T_TURN)
                if k == 3:
                    G = NG * b + g
                    dve.wait_ge(s["turn_ready"], G + 1)
                    heads = turn[:, :].rearrange("p (t h c) -> p t h c", t=NT, h=HG)
                    nc.vector.tensor_tensor(denom[:, :, :], heads[:, :, :, HD],
                                            over(exp_bias[:, HG * g:HG * (g + 1)]), ALU.add)\
                        .then_inc(s["denom_step"], 1)
                    dve.wait_ge(s["denom_step"], 2 * G + 1)
                    nc.vector.reciprocal(denom_inv[:, :, :], denom[:, :, :]).then_inc(s["denom_step"], 1)
                    if g == 0:
                        dve.wait_ge(s["oc_ps"], b)
                    dve.wait_ge(s["denom_step"], 2 * G + 2)
                    dst = o_tok[:, :, D // NG * g:D // NG * (g + 1)].rearrange("p t (h d) -> p t h d", h=HG)
                    nc.vector.tensor_tensor(dst, heads[:, :, :, 0:HD],
                                            denom_inv[:, :, :].unsqueeze(3).broadcast_to([P, NT, HG, HD]),
                                            ALU.mult).then_inc(s["o_norm"], 1)
                for n, (src, ready) in enumerate(((x_in[:, q], "x_loaded"), (x1, "x1_done"), (x2, "x2_done"),
                                                  (x3, "x3_done"))):
                    start = (T_LN0, T_LN1, T_LN2, T_LN3)[n]
                    if T in (start, start + 1):
                        if T == start:
                            dve.wait_ge(s[ready], (16 if n == 0 else 1) * (b + 1))
                        ln_stats(n, b, src, T - start)
                    start = (T_HAT0, T_HAT1, T_HAT2, T_HAT3)[n]
                    if T in (start, start + 1):
                        normalize(n, b, src, T - start)
                if T == T_SUM:
                    dve.wait_ge(s["h_sq_done"], b + 1)
                    nc.vector.tensor_reduce(h_sum[:, :], h_sq[:, :, :], AX_X, ALU.add)\
                        .then_inc(s["h_sum_done"], 1)
                elif T == T_SCAN:
                    dve.wait_ge(s["dt_done"], b + 1)
                    nc.vector.tensor_scalar(keep[:, :], dt_tanh[:, :], -0.5, 0.5, ALU.mult, ALU.add)\
                        .then_inc(s["scan_step"], 1)
                    dve.wait_ge(s["ut_done"], b + 1)
                    nc.vector.scalar_tensor_tensor(feed[:, :], dt_tanh[:, :], 1.0, u_tanh[:, :], ALU.add,
                                                   ALU.mult).then_inc(s["scan_step"], 1)
                elif T == T_SCAN + 1:
                    dve.wait_ge(s["scan_step"], 3 * b + 2)
                    nc.vector.tensor_tensor_scan(state[:, :], keep[:, :], feed[:, :], 0.0, ALU.mult, ALU.add)\
                        .then_inc(s["scan_step"], 1)
                elif T == T_SCAN + 2:
                    dve.wait_ge(s["scan_step"], 3 * b + 3)
                    dve.wait_ge(s["g_done"], b + 1)
                    nc.vector.scalar_tensor_tensor(y[0:S, :], g_tanh[:, :], 1.0, state[:, :], ALU.add,
                                                   ALU.mult).then_inc(s["y_done"], 1)
                elif T == T_X1 + 1:
                    dve.wait_ge(s["xh_done"], b + 1)
                    dve.wait_ge(s["out_ps"], b + 1)
                    nc.vector.tensor_tensor(x1[:, :, :], x_in[:, q], tiles(front[:, :]), ALU.add)\
                        .then_inc(s["x1_done"], 1)
                elif T == T_MIX0:
                    mix(0, b, mix_r, 0)
                elif T == T_MIX0 + 1:
                    mix(0, b, mix_k, 1)
                elif T == T_KV0 + 1:
                    ffn_gate(0, b, front)
                elif T == T_X3 + 1:
                    dve.wait_ge(s["out_stored"], 16 * (b + 1))
                    dve.wait_ge(s["xbo_done"], b + 1)
                    dve.wait_ge(s["wo_ps"], b + 1)
                    nc.vector.tensor_tensor(x3[:, :, :], x_bo[:, q], tiles(end[:, :]), ALU.add)\
                        .then_inc(s["x3_done"], 1)
                elif T == T_MIX1:
                    mix(1, b, mix_r, 0)
                elif T == T_MIX1 + 1:
                    mix(1, b, mix_k, 1)
                elif T == T_KV1 + 1:
                    ffn_gate(1, b, end)

            iterations(dve, stage)


N_WEIGHTS = 9 + 4 + 2 + 2 * 5

_INS = ["L0_attn_x", "L0_attn_W_in", "L0_attn_w_norm", "L0_attn_b_in", "L0_attn_W_x", "L0_attn_b_x",
        "L0_attn_W_dt", "L0_attn_b_dt", "L0_attn_W_out", "L0_attn_b_out"]
_FFN = ["W_r", "W_k", "W_v", "mu_r", "mu_k"]
_TURNED = ("W_r", "W_k", "W_v", "Wq", "Wk", "Wv", "Wo", "_c")


def kernel(**inputs):
    import numpy as _np
    import concourse.bacc as _bacc
    from concourse import mybir as _mybir
    from concourse.bass_utils import run_bass_kernel_spmd as _run

    nc = _bacc.Bacc("TRN2", target_bir_lowering=False, num_devices=1)
    arrays = {}

    def give(name):
        a = _np.asarray(inputs[name])
        if name.endswith(("Wq", "Wk")):
            a = a.reshape(H, HD, D).transpose(1, 0, 2).reshape(D, D)
        if name.endswith(_TURNED):
            a = a.T
        a = _np.ascontiguousarray(a)
        arrays[f"in_{name}"] = a
        return nc.dram_tensor(f"in_{name}", a.shape, _mybir.dt.from_np(a.dtype), kind="ExternalInput").ap()

    layer0 = [give(n) for n in _INS]
    f0 = [give(f"L0_ffn_{n}") for n in _FFN]
    c0, wmod0 = give("L0_c"), give("L0_wmod")
    attn = [give(f"L1_attn_{n}") for n in ("Wq", "Wk", "Wv", "Wo", "bo", "denom_bias")]
    f1 = [give(f"L1_ffn_{n}") for n in _FFN]
    c1, wmod1 = give("L1_c"), give("L1_wmod")
    out = nc.dram_tensor("out", (NB, L, D), F32, kind="ExternalOutput").ap()
    build(nc, *layer0, f0, c0, wmod0, *attn, f1, c1, wmod1, out)
    r = _run(nc, [arrays], core_ids=[0])
    return r.results[0]["out"]
```
